# Optimizing a Trainium2 kernel written in Bass

```python
import numpy as np
import jax
import jax.numpy as jnp

def _softmax(x, axis=-1):
    return jax.nn.softmax(x, axis=axis)

def _gelu(x):
    return jax.nn.gelu(x, approximate=True)

def _silu(x):
    return jax.nn.silu(x)

def _sigmoid(x):
    return jax.nn.sigmoid(x)

def _layernorm(x, axis=-1, eps=1e-05):
    m = jnp.mean(x, axis=axis, keepdims=True)
    v = jnp.var(x, axis=axis, keepdims=True)
    return (x - m) / jnp.sqrt(v + eps)

def _scatter_add(tgt, idx, src, axis=0):
    return tgt.at[idx].add(src)

def _segment_sum(src, seg, n):
    return jax.ops.segment_sum(src, seg, n)
kernel_name = 'mk_dlrm_tower_d1_rec_r8_dc53af'

def setup_inputs(seed: int=0):
    np.random.seed(seed)
    _w = jnp.asarray

    def _rec_inputs():
        import jax
        import jax.numpy as jnp
        _tk = jax.random.key(seed)
        dense_ctx = jax.random.normal(jax.random.fold_in(_tk, 190), (1024, 16), jnp.float32)
        ids = jnp.stack([jax.random.randint(jax.random.fold_in(_tk, 200 + f), (1024,), 0, v, jnp.int32) for f, v in enumerate([12500, 1000, 125000, 125000, 1250, 12500, 1250, 12500, 125000, 1250, 125000, 1250, 1000, 1000, 1000, 1250, 12500, 125000, 12500, 1000, 12500, 1000, 1000, 1250, 12500, 125000, 1250, 12500, 12500, 1000, 1000, 125000, 12500, 1000, 1250, 1250, 1250, 1000, 125000])], axis=1)
        tbl_0 = 0.05 * jax.random.normal(jax.random.fold_in(_tk, 500 + 0), (12500, 16), jnp.float32)
        tbl_1 = 0.05 * jax.random.normal(jax.random.fold_in(_tk, 500 + 1), (1000, 16), jnp.float32)
        tbl_2 = 0.05 * jax.random.normal(jax.random.fold_in(_tk, 500 + 2), (125000, 16), jnp.float32)
        tbl_3 = 0.05 * jax.random.normal(jax.random.fold_in(_tk, 500 + 3), (125000, 16), jnp.float32)
        tbl_4 = 0.05 * jax.random.normal(jax.random.fold_in(_tk, 500 + 4), (1250, 16), jnp.float32)
        tbl_5 = 0.05 * jax.random.normal(jax.random.fold_in(_tk, 500 + 5), (12500, 16), jnp.float32)
        tbl_6 = 0.05 * jax.random.normal(jax.random.fold_in(_tk, 500 + 6), (1250, 16), jnp.float32)
        tbl_7 = 0.05 * jax.random.normal(jax.random.fold_in(_tk, 500 + 7), (12500, 16), jnp.float32)
        tbl_8 = 0.05 * jax.random.normal(jax.random.fold_in(_tk, 500 + 8), (125000, 16), jnp.float32)
        tbl_9 = 0.05 * jax.random.normal(jax.random.fold_in(_tk, 500 + 9), (1250, 16), jnp.float32)
        tbl_10 = 0.05 * jax.random.normal(jax.random.fold_in(_tk, 500 + 10), (125000, 16), jnp.float32)
        tbl_11 = 0.05 * jax.random.normal(jax.random.fold_in(_tk, 500 + 11), (1250, 16), jnp.float32)
        tbl_12 = 0.05 * jax.random.normal(jax.random.fold_in(_tk, 500 + 12), (1000, 16), jnp.float32)
        tbl_13 = 0.05 * jax.random.normal(jax.random.fold_in(_tk, 500 + 13), (1000, 16), jnp.float32)
        tbl_14 = 0.05 * jax.random.normal(jax.random.fold_in(_tk, 500 + 14), (1000, 16), jnp.float32)
        tbl_15 = 0.05 * jax.random.normal(jax.random.fold_in(_tk, 500 + 15), (1250, 16), jnp.float32)
        tbl_16 = 0.05 * jax.random.normal(jax.random.fold_in(_tk, 500 + 16), (12500, 16), jnp.float32)
        tbl_17 = 0.05 * jax.random.normal(jax.random.fold_in(_tk, 500 + 17), (125000, 16), jnp.float32)
        tbl_18 = 0.05 * jax.random.normal(jax.random.fold_in(_tk, 500 + 18), (12500, 16), jnp.float32)
        tbl_19 = 0.05 * jax.random.normal(jax.random.fold_in(_tk, 500 + 19), (1000, 16), jnp.float32)
        tbl_20 = 0.05 * jax.random.normal(jax.random.fold_in(_tk, 500 + 20), (12500, 16), jnp.float32)
        tbl_21 = 0.05 * jax.random.normal(jax.random.fold_in(_tk, 500 + 21), (1000, 16), jnp.float32)
        tbl_22 = 0.05 * jax.random.normal(jax.random.fold_in(_tk, 500 + 22), (1000, 16), jnp.float32)
        tbl_23 = 0.05 * jax.random.normal(jax.random.fold_in(_tk, 500 + 23), (1250, 16), jnp.float32)
        tbl_24 = 0.05 * jax.random.normal(jax.random.fold_in(_tk, 500 + 24), (12500, 16), jnp.float32)
        tbl_25 = 0.05 * jax.random.normal(jax.random.fold_in(_tk, 500 + 25), (125000, 16), jnp.float32)
        tbl_26 = 0.05 * jax.random.normal(jax.random.fold_in(_tk, 500 + 26), (1250, 16), jnp.float32)
        tbl_27 = 0.05 * jax.random.normal(jax.random.fold_in(_tk, 500 + 27), (12500, 16), jnp.float32)
        tbl_28 = 0.05 * jax.random.normal(jax.random.fold_in(_tk, 500 + 28), (12500, 16), jnp.float32)
        tbl_29 = 0.05 * jax.random.normal(jax.random.fold_in(_tk, 500 + 29), (1000, 16), jnp.float32)
        tbl_30 = 0.05 * jax.random.normal(jax.random.fold_in(_tk, 500 + 30), (1000, 16), jnp.float32)
        tbl_31 = 0.05 * jax.random.normal(jax.random.fold_in(_tk, 500 + 31), (125000, 16), jnp.float32)
        tbl_32 = 0.05 * jax.random.normal(jax.random.fold_in(_tk, 500 + 32), (12500, 16), jnp.float32)
        tbl_33 = 0.05 * jax.random.normal(jax.random.fold_in(_tk, 500 + 33), (1000, 16), jnp.float32)
        tbl_34 = 0.05 * jax.random.normal(jax.random.fold_in(_tk, 500 + 34), (1250, 16), jnp.float32)
        tbl_35 = 0.05 * jax.random.normal(jax.random.fold_in(_tk, 500 + 35), (1250, 16), jnp.float32)
        tbl_36 = 0.05 * jax.random.normal(jax.random.fold_in(_tk, 500 + 36), (1250, 16), jnp.float32)
        tbl_37 = 0.05 * jax.random.normal(jax.random.fold_in(_tk, 500 + 37), (1000, 16), jnp.float32)
        tbl_38 = 0.05 * jax.random.normal(jax.random.fold_in(_tk, 500 + 38), (125000, 16), jnp.float32)
        _rk = jax.random.fold_in(_tk, 7)
        W_top1 = 0.05 * jax.random.normal(jax.random.fold_in(_tk, 801), (400, 512), jnp.float32)
        W_top2 = 0.0441942 * jax.random.normal(jax.random.fold_in(_tk, 802), (512, 256), jnp.float32)
        W_top3 = 0.0625 * jax.random.normal(jax.random.fold_in(_tk, 803), (256, 1), jnp.float32)
        b_top1 = jnp.zeros((512,), jnp.float32)
        b_top2 = jnp.zeros((256,), jnp.float32)
        return (dense_ctx, ids, tbl_0, tbl_1, tbl_2, tbl_3, tbl_4, tbl_5, tbl_6, tbl_7, tbl_8, tbl_9, tbl_10, tbl_11, tbl_12, tbl_13, tbl_14, tbl_15, tbl_16, tbl_17, tbl_18, tbl_19, tbl_20, tbl_21, tbl_22, tbl_23, tbl_24, tbl_25, tbl_26, tbl_27, tbl_28, tbl_29, tbl_30, tbl_31, tbl_32, tbl_33, tbl_34, tbl_35, tbl_36, tbl_37, tbl_38, W_top1, b_top1, W_top2, b_top2, W_top3)
    dense_ctx, ids, tbl_0, tbl_1, tbl_2, tbl_3, tbl_4, tbl_5, tbl_6, tbl_7, tbl_8, tbl_9, tbl_10, tbl_11, tbl_12, tbl_13, tbl_14, tbl_15, tbl_16, tbl_17, tbl_18, tbl_19, tbl_20, tbl_21, tbl_22, tbl_23, tbl_24, tbl_25, tbl_26, tbl_27, tbl_28, tbl_29, tbl_30, tbl_31, tbl_32, tbl_33, tbl_34, tbl_35, tbl_36, tbl_37, tbl_38, W_top1, b_top1, W_top2, b_top2, W_top3 = _rec_inputs()

    def _L0_rec_setup():
        import jax, jax.numpy as jnp
        import numpy as np
        B, F0, D = (512, 39, 16)
        CIN = [128, 128, 128]

        def _cin_layer(X0, Xi, W, b):
            H = W.shape[0]
            F0_, Fi = (X0.shape[1], Xi.shape[1])
            Wr = W.reshape(H, F0_, Fi)
            return jnp.einsum('hjk,bjd,bkd->bhd', Wr, X0, Xi) + b[None, :, None]
        key = jax.random.key(seed)
        ks = jax.random.split(key, 4)
        x = jax.random.normal(ks[0], (B, F0, D), dtype=jnp.float32)
        fields = [F0] + CIN
        inp = {'embedded_features': x}
        for i in range(len(CIN)):
            cin = F0 * fields[i]
            cout = fields[i + 1]
            kw = jax.random.fold_in(ks[1], i)
            inp[f'W{i}'] = jax.random.normal(kw, (cout, cin), dtype=jnp.float32) / np.sqrt(cin)
            inp[f'b{i}'] = jnp.zeros((cout,), dtype=jnp.float32)
        return inp
    _L0_rec_all = _L0_rec_setup()
    _L0_rec_in = {k: v for k, v in _L0_rec_all.items() if k in ('W0', 'b0', 'W1', 'b1', 'W2', 'b2')}
    del _L0_rec_all
    return {'dense_ctx': dense_ctx, 'ids': ids, 'tbl_0': tbl_0, 'tbl_1': tbl_1, 'tbl_2': tbl_2, 'tbl_3': tbl_3, 'tbl_4': tbl_4, 'tbl_5': tbl_5, 'tbl_6': tbl_6, 'tbl_7': tbl_7, 'tbl_8': tbl_8, 'tbl_9': tbl_9, 'tbl_10': tbl_10, 'tbl_11': tbl_11, 'tbl_12': tbl_12, 'tbl_13': tbl_13, 'tbl_14': tbl_14, 'tbl_15': tbl_15, 'tbl_16': tbl_16, 'tbl_17': tbl_17, 'tbl_18': tbl_18, 'tbl_19': tbl_19, 'tbl_20': tbl_20, 'tbl_21': tbl_21, 'tbl_22': tbl_22, 'tbl_23': tbl_23, 'tbl_24': tbl_24, 'tbl_25': tbl_25, 'tbl_26': tbl_26, 'tbl_27': tbl_27, 'tbl_28': tbl_28, 'tbl_29': tbl_29, 'tbl_30': tbl_30, 'tbl_31': tbl_31, 'tbl_32': tbl_32, 'tbl_33': tbl_33, 'tbl_34': tbl_34, 'tbl_35': tbl_35, 'tbl_36': tbl_36, 'tbl_37': tbl_37, 'tbl_38': tbl_38, 'W_top1': W_top1, 'b_top1': b_top1, 'W_top2': W_top2, 'b_top2': b_top2, 'W_top3': W_top3, 'L0_rec_W0': _L0_rec_in['W0'], 'L0_rec_b0': _L0_rec_in['b0'], 'L0_rec_W1': _L0_rec_in['W1'], 'L0_rec_b1': _L0_rec_in['b1'], 'L0_rec_W2': _L0_rec_in['W2'], 'L0_rec_b2': _L0_rec_in['b2']}

def reference(dense_ctx, ids, tbl_0, tbl_1, tbl_2, tbl_3, tbl_4, tbl_5, tbl_6, tbl_7, tbl_8, tbl_9, tbl_10, tbl_11, tbl_12, tbl_13, tbl_14, tbl_15, tbl_16, tbl_17, tbl_18, tbl_19, tbl_20, tbl_21, tbl_22, tbl_23, tbl_24, tbl_25, tbl_26, tbl_27, tbl_28, tbl_29, tbl_30, tbl_31, tbl_32, tbl_33, tbl_34, tbl_35, tbl_36, tbl_37, tbl_38, W_top1, b_top1, W_top2, b_top2, W_top3, L0_rec_W0, L0_rec_b0, L0_rec_W1, L0_rec_b1, L0_rec_W2, L0_rec_b2):
    import jax
    import jax.numpy as jnp

    def _L0_rec_ref(embedded_features, W0, b0, W1, b1, W2, b2):
        import jax, jax.numpy as jnp
        import numpy as np
        B, F0, D = (512, 39, 16)
        CIN = [128, 128, 128]

        def _cin_layer(X0, Xi, W, b):
            H = W.shape[0]
            F0_, Fi = (X0.shape[1], Xi.shape[1])
            Wr = W.reshape(H, F0_, Fi)
            return jnp.einsum('hjk,bjd,bkd->bhd', Wr, X0, Xi) + b[None, :, None]
        X0 = embedded_features
        Ws = [(W0, b0), (W1, b1), (W2, b2)]
        Xi = X0
        res = []
        for W, b in Ws:
            Xi = _cin_layer(X0, Xi, W, b)
            res.append(Xi.sum(axis=2))
        return jnp.concatenate(res, axis=1)
    e = jnp.stack([tbl_0[ids[:, 0]], tbl_1[ids[:, 1]], tbl_2[ids[:, 2]], tbl_3[ids[:, 3]], tbl_4[ids[:, 4]], tbl_5[ids[:, 5]], tbl_6[ids[:, 6]], tbl_7[ids[:, 7]], tbl_8[ids[:, 8]], tbl_9[ids[:, 9]], tbl_10[ids[:, 10]], tbl_11[ids[:, 11]], tbl_12[ids[:, 12]], tbl_13[ids[:, 13]], tbl_14[ids[:, 14]], tbl_15[ids[:, 15]], tbl_16[ids[:, 16]], tbl_17[ids[:, 17]], tbl_18[ids[:, 18]], tbl_19[ids[:, 19]], tbl_20[ids[:, 20]], tbl_21[ids[:, 21]], tbl_22[ids[:, 22]], tbl_23[ids[:, 23]], tbl_24[ids[:, 24]], tbl_25[ids[:, 25]], tbl_26[ids[:, 26]], tbl_27[ids[:, 27]], tbl_28[ids[:, 28]], tbl_29[ids[:, 29]], tbl_30[ids[:, 30]], tbl_31[ids[:, 31]], tbl_32[ids[:, 32]], tbl_33[ids[:, 33]], tbl_34[ids[:, 34]], tbl_35[ids[:, 35]], tbl_36[ids[:, 36]], tbl_37[ids[:, 37]], tbl_38[ids[:, 38]]], axis=1)
    z = _L0_rec_ref(e, L0_rec_W0, L0_rec_b0, L0_rec_W1, L0_rec_b1, L0_rec_W2, L0_rec_b2)
    z = z.reshape(z.shape[0], -1)
    h = jnp.concatenate([z, dense_ctx], axis=1)
    h = jnp.maximum(h @ W_top1 + b_top1, 0.0)
    h = jnp.maximum(h @ W_top2 + b_top2, 0.0)
    y = h @ W_top3
    return y

_drawn_inputs = setup_inputs


def setup_inputs(seed=0):
    import zlib

    import numpy as np

    out = dict(_drawn_inputs(seed))
    spreads = {'b_top1': (0.0, 0.1),
     'b_top2': (0.0, 0.1),
     'L0_rec_b0': (0.0, 0.1),
     'L0_rec_b1': (0.0, 0.1),
     'L0_rec_b2': (0.0, 0.1)}
    factors = {'tbl_0': 8.0,
     'tbl_1': 5.869,
     'tbl_2': 5.282,
     'tbl_3': 7.022,
     'tbl_4': 8.0,
     'tbl_5': 8.0,
     'tbl_6': 8.0,
     'tbl_7': 6.78,
     'tbl_8': 8.0,
     'tbl_9': 8.0,
     'tbl_10': 8.0,
     'tbl_11': 6.612,
     'tbl_12': 8.0,
     'tbl_13': 8.0,
     'tbl_14': 4.264,
     'tbl_15': 5.74,
     'tbl_16': 8.0,
     'tbl_17': 8.0,
     'tbl_18': 8.0,
     'tbl_19': 5.677,
     'tbl_20': 7.234,
     'tbl_21': 8.0,
     'tbl_22': 8.0,
     'tbl_23': 8.0,
     'tbl_24': 8.0,
     'tbl_25': 7.352,
     'tbl_26': 5.853,
     'tbl_27': 8.0,
     'tbl_28': 8.0,
     'tbl_29': 8.0,
     'tbl_30': 6.425,
     'tbl_31': 6.542,
     'tbl_32': 8.0,
     'tbl_33': 6.294,
     'tbl_34': 8.0,
     'tbl_35': 7.615,
     'tbl_36': 8.0,
     'tbl_37': 6.68,
     'tbl_38': 8.0,
     'L0_rec_W0': 3.007}
    for name, (base, spread) in spreads.items():
        noise = np.random.default_rng([zlib.crc32(name.encode()), seed]).standard_normal(out[name].shape)
        drawn = base * np.exp(spread * noise) if base else spread * noise
        out[name] = jnp.asarray(drawn.astype(out[name].dtype))
    for name, factor in factors.items():
        out[name] = (out[name] * factor).astype(out[name].dtype)
    return out
```

```python
from contextlib import ExitStack

import concourse.bass as bass
from concourse import mybir

B, F, D, H = 1024, 39, 16, 128
P = 128
BLOCK_B = P // D
BLOCKS = B // BLOCK_B
SUPER = 4
SUPERS = BLOCKS // SUPER
PAIRS = SUPERS // 2
PAIR_BLOCKS = 2 * SUPER
GROUP_B = 128
GROUPS = B // GROUP_B
GROUP_BLOCKS = GROUP_B // BLOCK_B
LAG = 2
BANK = 512

RS = (F + 1) // 2
R_TILE = 3
TILES = -(-RS // R_TILE)
TILE_R = [min(R_TILE, RS - R_TILE * t) for t in range(TILES)]
SLOT_TILES = [[0, 1], [2, 3], [4, 5], [6]]

CHUNK_J = 4
CHUNKS = -(-F // CHUNK_J)
T_BANKS = 4
DVE_CHUNKS = [0, 2, 3, 5, 7, 8]
ACT_CHUNKS = [1, 4, 6, 9]
MACS = CHUNK_J * len(DVE_CHUNKS)
FOLDS = 6
FOLD_READ = [1, 1, 2, 3]

ROW = 60
EXT = F + RS - 1
GC = F + 1
BD_W = BLOCK_B * GC

H1, H2 = 512, 256
ZPAD = LAG * BLOCK_B
GATHER_A = 20
GATHER_B = F - GATHER_A


def chunk_fields(c):
    return min(CHUNK_J, F - CHUNK_J * c)


def wait(engine, semaphore, value):
    if isinstance(value, int) and value <= 0:
        return
    engine.wait_ge(semaphore, value)


def t_consumer(k_local):
    n, c = divmod(k_local, CHUNKS)
    if c in DVE_CHUNKS:
        return "dve", MACS * n + CHUNK_J * (DVE_CHUNKS.index(c) + 1)
    return "act", len(ACT_CHUNKS) * n + ACT_CHUNKS.index(c) + 1


def dlrm_cin_tower(nc, dense_t, ids, tables, w_top1, b_top1, w_top2, b_top2, w_top3,
                   w0_a, w0_b, b0, w1_t, b1, w2_t, b2, out):
    f32, f32r, i32 = mybir.dt.float32, mybir.dt.float32r, mybir.dt.int32
    ALU, ACT = mybir.AluOpType, mybir.ActivationFunctionType
    AX = mybir.AxisListType

    rows_dram = nc.dram_tensor("x0_rows", ((GROUPS + 1) * GROUP_B * D, ROW), f32)[:, :]
    rows_by_block = rows_dram.rearrange("(n p) c -> p n c", p=P)
    rows_by_group = rows_dram.rearrange("(g b d) c -> b g (d c)", b=GROUP_B, d=D)

    ctx = ExitStack()
    with ctx:
        def sb(name, shape, dt=f32):
            return ctx.enter_context(nc.sbuf_tensor(name, shape, dt))

        def sem(name):
            return ctx.enter_context(nc.semaphore(name))

        w1_hi, w1_lo = sb("w1_hi", [P, F * H], f32r), sb("w1_lo", [P, F * H], f32r)
        w2 = sb("w2", [P, F, H])
        w0_hi, w0_lo = sb("w0_hi", [P, TILES, H], f32r), sb("w0_lo", [P, TILES, H], f32r)
        wt1 = sb("wt1", [P, 4, H1])
        wt2 = sb("wt2", [P, 4, H2])
        wt3 = sb("wt3", [P, 2])
        bt1, bt2 = sb("bt1", [P, 4]), sb("bt2", [P, 2])
        b_cin = sb("b_cin", [P, 2])
        b_cin16 = sb("b_cin16", [P, 2])
        acc_start = sb("acc_start", [P, CHUNK_J, H])
        dense = sb("dense", [D, B])
        ident = sb("ident", [P, P])
        ids_all = sb("ids_all", [P, GROUPS + 1, F], i32)
        idx_a, idx_b = sb("idx_a", [P, GATHER_A], i32), sb("idx_b", [P, GATHER_B], i32)
        emb = sb("emb", [P, F, D])
        rows = sb("rows", [P, D, ROW])
        x_pairs = [sb(f"x_pairs{i}", [P, SUPER, EXT]) for i in range(2)]
        x_scale = [sb(f"x_scale{i}", [P, SUPER, F]) for i in range(2)]
        x_diag = [sb(f"x_diag{i}", [P, SUPER, BD_W]) for i in range(2)]
        prod = [sb(f"prod{i}", [P, SUPER, R_TILE * F]) for i in range(2)]
        pt_hi = [sb(f"pt_hi{i}", [P, BANK], f32r) for i in range(2)]
        pt_lo = [sb(f"pt_lo{i}", [P, BANK], f32r) for i in range(2)]
        x1_hi = [sb(f"x1_hi{i}", [P, BANK], f32r) for i in range(2)]
        x1_lo = [sb(f"x1_lo{i}", [P, BANK], f32r) for i in range(2)]
        acc = [sb(f"acc{i}", [P, CHUNK_J, H]) for i in range(2)]
        scaled = [sb(f"scaled{i}", [P, CHUNK_J * H]) for i in range(len(ACT_CHUNKS))]
        fold = sb("fold", [P, CHUNK_J * H])
        x2 = [sb(f"x2_{i}", [P, H]) for i in range(2)]
        g_all = sb("g_all", [P, GC, GROUP_B])
        z0 = sb("z0", [P, B])
        z1, z2 = sb("z1", [P, ZPAD + B]), sb("z2", [P, ZPAD + B])
        h1 = sb("h1", [P, 4, B])
        h2 = sb("h2", [P, 2, B])
        y = sb("y", [1, B])
        W1_PART = F * H // 4
        w1_stage = [h1[:, :, :].rearrange("p a b -> p (a b)")[:, i * W1_PART:(i + 1) * W1_PART]
                    for i in range(3)] + [h2[:, :, :].rearrange("p a b -> p (a b)")[:, 0:W1_PART]]
        w0_stage_a, w0_stage_b = z1[:, 0:TILES * H], z2[:, 0:TILES * H]
        w0_sum = z0[:, 0:TILES * H]

        t_bank = [ctx.enter_context(nc.psum_tensor(f"t_bank{i}", [P, BANK], f32)) for i in range(T_BANKS)]
        pt_bank = [ctx.enter_context(nc.psum_tensor(f"pt_bank{i}", [P, BANK], f32)) for i in range(2)]
        x1_bank = ctx.enter_context(nc.psum_tensor("x1_bank", [P, BANK], f32))
        g_bank = ctx.enter_context(nc.psum_tensor("g_bank", [P, BANK], f32))

        ids_loaded, w0_loaded = sem("ids_loaded"), sem("w0_loaded")
        w1_loaded = sem("w1_loaded")
        bias_loaded, start_loaded = sem("bias_loaded"), sem("start_loaded")
        w2_loaded, top_loaded = sem("w2_loaded"), sem("top_loaded")
        zeroed = sem("zeroed")
        idx_ready = sem("idx_ready")
        gathered_a, gathered_b = sem("gathered_a"), sem("gathered_b")
        rows_made, rows_stored = sem("rows_made"), sem("rows_stored")
        pairs_loaded = [sem("pairs_loaded0"), sem("pairs_loaded1")]
        scale_loaded = [sem("scale_loaded0"), sem("scale_loaded1")]
        diag_loaded = [sem("diag_loaded0"), sem("diag_loaded1")]
        b16_ready = sem("b16_ready")
        w0_summed, w_hi_ready, w_lo_ready = sem("w0_summed"), sem("w_hi_ready"), sem("w_lo_ready")
        prod_ready, tr_ready = sem("prod_ready"), sem("tr_ready")
        hi_ready, lo_ready = sem("hi_ready"), sem("lo_ready")
        l0_done = sem("l0_done")
        x1hi_ready, x1lo_ready, z0_ready = sem("x1hi_ready"), sem("x1lo_ready"), sem("z0_ready")
        t_ready = sem("t_ready")
        mac_done = sem("mac_done")
        scaled_ready = sem("scaled_ready")
        fold_step = sem("fold_step")
        g_ready, g_stored = sem("g_ready"), sem("g_stored")
        z1_stored = sem("z1_stored")
        z2_ready, z2_stored = sem("z2_ready"), sem("z2_stored")
        z0_biased = sem("z0_biased")
        h1_ready, h1_stored = sem("h1_ready"), sem("h1_stored")
        h2_ready, h2_stored = sem("h2_ready"), sem("h2_stored")
        y_ready, y_stored, y_written = sem("y_ready"), sem("y_stored"), sem("y_written")

        block = ctx.enter_context(nc.Block())

        def mlp_bank(i):
            return (t_bank + pt_bank + [x1_bank, g_bank])[i]

        def x_window(buf, t):
            base = buf[:, :, R_TILE * t:R_TILE * t + F]
            (ps, pn), (bs, bn), (js, jn) = base.ap
            return bass.AP(tensor=base.tensor, offset=base.offset,
                           ap=[[ps, pn], [bs, bn], [1, TILE_R[t]], [js, jn]])

        @block.sync
        def _(sp):
            sp.dma_start(ids_all[:, 0:GROUPS, :], ids.rearrange("(g p) f -> p g f", p=P)).then_inc(ids_loaded, 16)
            sp.dma_start(w0_stage_a, w0_a).then_inc(w0_loaded, 16)
            sp.dma_start(w0_stage_b, w0_b).then_inc(w0_loaded, 16)
            sp.dma_start(b_cin[:, 0:1], b0).then_inc(bias_loaded, 16)
            sp.dma_start(b_cin[:, 1:2], b2).then_inc(bias_loaded, 16)
            for i in range(4):
                sp.dma_start(w1_stage[i], w1_t[:, i * W1_PART:(i + 1) * W1_PART]).then_inc(w1_loaded, 16)
            sp.wait_ge(zeroed, 1)
            sp.dma_start(acc_start[:, 0, :], b1.partition_broadcast(P)).then_inc(start_loaded, 16)
            sp.dma_start(w2[:, :, :].rearrange("p j h -> p (j h)"), w2_t).then_inc(w2_loaded, 16)

            def load_pairs(s, par):
                sp.dma_start(x_pairs[par][:, :, :], rows_by_block[:, bass.ds(SUPER * s, SUPER), 1:1 + EXT])\
                  .then_inc(pairs_loaded[par], 16)

            def load_scale(s, par):
                sp.dma_start(x_scale[par][:, :, :], rows_by_block[:, bass.ds(SUPER * s, SUPER), 1:1 + F])\
                  .then_inc(scale_loaded[par], 16)

            def load_diag(s, par):
                for i in reversed(range(BLOCK_B)):
                    r = slice(D * i, D * (i + 1))
                    sp.dma_start(x_diag[par][r, :, GC * i:GC * (i + 1)],
                                 rows_by_block[r, bass.ds(SUPER * s, SUPER), 0:GC])\
                      .then_inc(diag_loaded[par], 16)

            def step(s, par, last):
                wait(sp, g_ready, SUPER * s)
                load_diag(s + 1, 1 - par)
                if last:
                    return
                wait(sp, prod_ready, TILES * (s + 1))
                wait(sp, rows_stored, row_stores(s + 2))
                load_pairs(s + 2, par)
                wait(sp, fold_step, FOLDS * SUPER * (s + 1))
                load_scale(s + 2, par)

            def row_stores(s):
                return 16 * (s // 4 + 1)

            sp.wait_ge(rows_stored, 16)
            sp.wait_ge(zeroed, 4)
            load_pairs(0, 0)
            load_scale(0, 0)
            load_diag(0, 0)
            load_pairs(1, 1)
            load_scale(1, 1)
            step(0, 0, False)
            step(1, 1, False)
            sp.dma_start(wt1[:, 0:3, :], w_top1[0:3 * P, :].rearrange("(t p) n -> p t n", p=P)).then_inc(top_loaded, 16)
            sp.dma_start(wt1[0:D, 3, :], w_top1[3 * P:3 * P + D, :]).then_inc(top_loaded, 16)
            sp.dma_start(wt2[:, :, :], w_top2.rearrange("(t p) n -> p t n", p=P)).then_inc(top_loaded, 16)
            sp.dma_start(wt3[:, :], w_top3).then_inc(top_loaded, 16)
            sp.dma_start(bt1[:, :], b_top1).then_inc(top_loaded, 16)
            sp.dma_start(bt2[:, :], b_top2).then_inc(top_loaded, 16)
            sp.dma_start(dense[:, :], dense_t).then_inc(top_loaded, 16)
            with sp.Fori(0, (SUPERS - 4) // 4) as g:
                for i in range(4):
                    s = 4 * g + 2 + i
                    wait(sp, g_ready, SUPER * s)
                    load_diag(s + 1, 1 - i % 2)
                    wait(sp, prod_ready, TILES * (s + 1))
                    wait(sp, rows_stored, 16 * g + 32)
                    load_pairs(s + 2, i % 2)
                    wait(sp, fold_step, FOLDS * SUPER * (s + 1))
                    load_scale(s + 2, i % 2)
            step(SUPERS - 2, 0, True)
            sp.wait_ge(y_stored, 1)
            sp.dma_start(out, y[:, :]).then_inc(y_written, 16)
            sp.wait_ge(y_written, 16)

        @block.gpsimd
        def _(pool):
            pool.memset(acc_start[:, :, :], 0.0).then_inc(zeroed, 1)
            pool.memset(ids_all[:, GROUPS, :], 0).then_inc(zeroed, 1)
            pool.wait_ge(ids_loaded, 16)

            def take_idx(dst, group, first, n, already):
                wait(pool, rows_made, already)
                pool.tensor_copy(dst[:, :], ids_all[:, bass.ds(group, 1), first:first + n]
                                 .rearrange("p g f -> p (g f)")).then_inc(idx_ready, 1)

            def gather(f):
                idx, at, done = (idx_a, f, gathered_a) if f < GATHER_A else (idx_b, f - GATHER_A, gathered_b)
                pool.indirect_dma_start(out=emb[:, f, :], out_offset=None, in_=tables[f],
                                        in_offset=bass.IndirectOffsetOnAxis(ap=idx[:, at:at + 1], axis=0))\
                    .then_inc(done, 16)

            take_idx(idx_a, 0, 0, GATHER_A, 0)
            take_idx(idx_b, 0, GATHER_A, GATHER_B, 0)
            pool.wait_ge(idx_ready, 2)
            for f in range(F):
                gather(f)
            pool.memset(rows[:, :, 0:1], 1.0)
            pool.memset(rows[:, :, ROW - 1:ROW], 0.0).then_inc(zeroed, 1)
            pool.memset(x_diag[0][:, :, :], 0.0)
            pool.memset(x_diag[1][:, :, :], 0.0).then_inc(zeroed, 1)
            pool.memset(ident[:, :], 0.0).then_inc(zeroed, 1)
            pool.wait_ge(zeroed, 5)
            pool.affine_select(out=ident[:, :], in_=ident[:, :], compare_op=ALU.not_equal, fill=1.0,
                               base=0, pattern=[[-1, P]], channel_multiplier=1).then_inc(zeroed, 1)
            pool.memset(g_all[:, :, 0:ZPAD], 0.0).then_inc(zeroed, 1)
            take_idx(idx_a, 1, 0, GATHER_A, 1)
            pool.wait_ge(idx_ready, 3)
            for f in range(GATHER_A):
                gather(f)

            def folds(n, nb):
                a = acc[nb % 2][:, :, :].rearrange("p c h -> p (c h)")
                s1, s2 = CHUNK_J * H // 2, CHUNK_J * H // 4
                w3 = chunk_fields(ACT_CHUNKS[3]) * H
                wait(pool, scaled_ready, 4 * n + 2)
                wait(pool, fold_step, FOLDS * n)
                pool.tensor_tensor(fold[:, :], scaled[0][:, :], scaled[1][:, :], ALU.add).then_inc(fold_step, 1)
                wait(pool, scaled_ready, 4 * n + 3)
                wait(pool, fold_step, FOLDS * n + 1)
                pool.tensor_tensor(fold[:, :], fold[:, :], scaled[2][:, :], ALU.add).then_inc(fold_step, 1)
                wait(pool, scaled_ready, 4 * n + 4)
                wait(pool, fold_step, FOLDS * n + 2)
                pool.tensor_tensor(fold[:, 0:w3], fold[:, 0:w3], scaled[3][:, 0:w3], ALU.add).then_inc(fold_step, 1)
                wait(pool, mac_done, MACS * (n + 1))
                wait(pool, fold_step, FOLDS * n + 3)
                pool.tensor_tensor(fold[:, :], fold[:, :], a, ALU.add).then_inc(fold_step, 1)
                wait(pool, fold_step, FOLDS * n + 4)
                pool.tensor_tensor(fold[:, 0:s1], fold[:, 0:s1], fold[:, s1:2 * s1], ALU.add).then_inc(fold_step, 1)
                wait(pool, fold_step, FOLDS * n + 5)
                wait(pool, g_ready, n - 1)
                pool.tensor_tensor(x2[nb % 2][:, :], fold[:, 0:s2], fold[:, s2:2 * s2], ALU.add).then_inc(fold_step, 1)

            def pair(p, lot, group):
                fields = {"a": list(range(GATHER_A)), "b": list(range(GATHER_A, F)), None: []}[lot]
                if lot == "a":
                    take_idx(idx_a, group, 0, GATHER_A, group)
                    wait(pool, idx_ready, 2 * group + 1)
                elif lot == "b":
                    take_idx(idx_b, group, GATHER_A, GATHER_B, group)
                    wait(pool, idx_ready, 2 * group + 2)
                for nb in range(PAIR_BLOCKS):
                    folds(PAIR_BLOCKS * p + nb, nb)
                    take = -(-len(fields) // (PAIR_BLOCKS - nb))
                    for f in fields[:take]:
                        gather(f)
                    fields = fields[take:]

            pair(0, "b", 1)
            with pool.Fori(0, GROUPS - 1) as g:
                pair(2 * g + 1, "a", g + 2)
                pair(2 * g + 2, "b", g + 2)
            pair(PAIRS - 1, None, None)
            pool.wait_ge(gathered_a, 16 * GATHER_A * (GROUPS + 1))
            pool.wait_ge(gathered_b, 16 * GATHER_B * (GROUPS + 1))

        @block.scalar
        def _(act):
            def store_rows(g):
                wait(act, gathered_a, 16 * GATHER_A * (g + 1))
                wait(act, gathered_b, 16 * GATHER_B * (g + 1))
                wait(act, rows_stored, 16 * g)
                nc.scalar.copy(rows[:, :, 1:1 + F], emb[:, :, :].rearrange("p f d -> p d f"))
                nc.scalar.copy(rows[:, :, 1 + F:1 + EXT], emb[:, 0:EXT - F, :].rearrange("p f d -> p d f"))\
                    .then_inc(rows_made, 1)
                wait(act, rows_made, g + 1)
                act.dma_start(rows_by_group[:, bass.ds(g, 1), :],
                              rows[:, :, :].rearrange("p d (o c) -> p o (d c)", o=1)).then_inc(rows_stored, 16)

            act.wait_ge(w0_summed, 1)
            nc.scalar.copy(w0_hi[:, :, :].rearrange("p t h -> p (t h)"), w0_sum).then_inc(w_hi_ready, 1)
            act.wait_ge(w1_loaded, 64)
            for i in range(4):
                nc.scalar.copy(w1_hi[:, i * W1_PART:(i + 1) * W1_PART], w1_stage[i]).then_inc(w_hi_ready, 1)
            act.wait_ge(zeroed, 3)
            store_rows(0)

            def tile_hi(u, par, t):
                wait(act, tr_ready, u + 1)
                wait(act, l0_done, u - 1)
                k = TILE_R[t] * F
                nc.scalar.copy(pt_hi[par][0:k, :], pt_bank[par][0:k, :]).then_inc(hi_ready, 1)

            def x1_high(s, par):
                wait(act, l0_done, TILES * (s + 1))
                wait(act, t_ready, CHUNKS * SUPER * (s - 1))
                nc.scalar.activation(x1_hi[par][:, :], x1_bank[:, :], ACT.Identity, bias=b_cin[:, 0:1])\
                    .then_inc(x1hi_ready, 1)

            def scale_chunk(n, nb, a):
                c = ACT_CHUNKS[a]
                par, q = nb // SUPER, nb % SUPER
                wait(act, t_ready, CHUNKS * n + c + 1)
                wait(act, fold_step, FOLDS * (n - 1) + FOLD_READ[a])
                for i in range(chunk_fields(c)):
                    j = CHUNK_J * c + i
                    last = nc.scalar.activation(scaled[a][:, i * H:(i + 1) * H],
                                                t_bank[(CHUNKS * nb + c) % T_BANKS][:, i * H:(i + 1) * H],
                                                ACT.Copy, scale=x_scale[par][:, q, j:j + 1])
                last.then_inc(scaled_ready, 1)

            def store_g(m, slot):
                wait(act, g_ready, m + 1)
                nc.scalar.copy(g_all[:, :, BLOCK_B * slot:BLOCK_B * (slot + 1)],
                               g_bank[:, 0:BD_W].rearrange("p (b c) -> p c b", c=GC)).then_inc(g_stored, 1)

            def pair(p, half, first=False, last=False):
                for nb in range(PAIR_BLOCKS):
                    n, par, q = PAIR_BLOCKS * p + nb, nb // SUPER, nb % SUPER
                    s = 2 * p + par
                    tiles = [] if last and par else SLOT_TILES[q]
                    u0 = TILES * (s + 1)
                    if q == 0:
                        wait(act, scale_loaded[par], 16 * (p + 1))
                    if tiles:
                        tile_hi(u0 + tiles[0], (TILES * (1 - par) + tiles[0]) % 2, tiles[0])
                    scale_chunk(n, nb, 0)
                    if len(tiles) > 1:
                        tile_hi(u0 + tiles[1], (TILES * (1 - par) + tiles[1]) % 2, tiles[1])
                    if q == SUPER - 1 and tiles:
                        x1_high(s + 1, 1 - par)
                    scale_chunk(n, nb, 1)
                    if not (first and nb < LAG):
                        store_g(n - LAG, PAIR_BLOCKS * half + nb)
                    scale_chunk(n, nb, 2)
                    scale_chunk(n, nb, 3)

            def store_z(g, lo, width, stored):
                wait(act, g_stored, stored)
                nc.scalar.copy(z1[:, bass.ds(lo, width)], g_all[:, 0, 0:width]).then_inc(z1_stored, 1)
                wait(act, z2_ready, g + 1)
                nc.scalar.activation(z2[:, bass.ds(lo, width)], g_bank[:, 0:width], ACT.Identity,
                                     bias=b_cin16[:, 1:2]).then_inc(z2_stored, 1)

            act.wait_ge(bias_loaded, 32)
            act.wait_ge(w_lo_ready, 5)
            for t in range(TILES):
                tile_hi(t, t % 2, t)
            x1_high(0, 0)
            act.wait_ge(zeroed, 7)
            act.wait_ge(b16_ready, 1)
            pair(0, 0, first=True)
            store_rows(1)
            with act.Fori(0, GROUPS - 1) as g:
                pair(2 * g + 1, 1)
                store_z(g, GROUP_B * g, GROUP_B, GROUP_BLOCKS * (g + 1) - LAG)
                pair(2 * g + 2, 0)
                store_rows(g + 2)
            pair(PAIRS - 1, 1, last=True)
            store_z(GROUPS - 1, GROUP_B * (GROUPS - 1), GROUP_B, GROUP_BLOCKS * GROUPS - LAG)
            for i in range(LAG):
                store_g(BLOCKS - LAG + i, i)
            store_z(GROUPS, B, ZPAD, BLOCKS)
            act.wait_ge(z0_ready, SUPERS)
            nc.scalar.activation(z0[:, :], z0[:, :], ACT.Identity, bias=b_cin16[:, 0:1]).then_inc(z0_biased, 1)
            act.wait_ge(top_loaded, 16 * 7)
            for i in range(8):
                half, m = divmod(i, 4)
                act.wait_ge(h1_ready, i + 1)
                nc.scalar.activation(h1[:, m, half * BANK:(half + 1) * BANK], mlp_bank(i)[:, :], ACT.Relu,
                                     bias=bt1[:, m:m + 1]).then_inc(h1_stored, 1)
            for i in range(4):
                half, m = divmod(i, 2)
                act.wait_ge(h2_ready, i + 1)
                nc.scalar.activation(h2[:, m, half * BANK:(half + 1) * BANK], mlp_bank(i)[:, :], ACT.Relu,
                                     bias=bt2[:, m:m + 1]).then_inc(h2_stored, 1)
            act.wait_ge(y_ready, 1)
            nc.scalar.copy(y[:, 0:BANK], mlp_bank(4)[0:1, :])
            nc.scalar.copy(y[:, BANK:B], mlp_bank(5)[0:1, :]).then_inc(y_stored, 1)
            act.wait_ge(rows_stored, 16 * (GROUPS + 1))

        @block.vector
        def _(dve):
            dve.wait_ge(bias_loaded, 32)
            nc.vector.tensor_scalar(b_cin16[:, :], b_cin[:, :], float(D), None, ALU.mult).then_inc(b16_ready, 1)
            dve.wait_ge(w0_loaded, 32)
            nc.vector.tensor_tensor(w0_sum, w0_stage_a, w0_stage_b, ALU.add).then_inc(w0_summed, 1)
            dve.wait_ge(w0_summed, 1)
            dve.wait_ge(w_hi_ready, 1)
            nc.vector.tensor_tensor(w0_lo[:, :, :].rearrange("p t h -> p (t h)"), w0_sum,
                                    w0_hi[:, :, :].rearrange("p t h -> p (t h)").bitcast(f32),
                                    ALU.subtract).then_inc(w_lo_ready, 1)
            for i in range(4):
                part = slice(i * W1_PART, (i + 1) * W1_PART)
                dve.wait_ge(w_hi_ready, i + 2)
                nc.vector.tensor_tensor(w1_lo[:, part], w1_stage[i], w1_hi[:, part].bitcast(f32),
                                        ALU.subtract).then_inc(w_lo_ready, 1)

            def product(par, t, u, loads):
                if t == 0:
                    wait(dve, pairs_loaded[par], 16 * loads)
                wait(dve, tr_ready, u - 1)
                r = TILE_R[t]
                a = x_pairs[par][:, :, 0:F].unsqueeze(2).to_broadcast([P, SUPER, r, F])
                upar = (TILES * par + t) % 2
                nc.vector.tensor_tensor(prod[upar][:, :, 0:r * F].rearrange("p q (r j) -> p q r j", r=r),
                                        a, x_window(x_pairs[par], t), ALU.mult).then_inc(prod_ready, 1)

            def tile_lo(u, par, t):
                wait(dve, hi_ready, u + 1)
                wait(dve, l0_done, u - 1)
                k = TILE_R[t] * F
                nc.vector.tensor_tensor(pt_lo[par][0:k, :], pt_bank[par][0:k, :], pt_hi[par][0:k, :].bitcast(f32),
                                        ALU.subtract).then_inc(lo_ready, 1)

            def x1_low(s, par):
                wait(dve, x1hi_ready, s + 1)
                nc.vector.scalar_tensor_tensor(x1_lo[par][:, :], x1_bank[:, :], b_cin[:, 0:1],
                                               x1_hi[par][:, :].bitcast(f32), ALU.add, ALU.subtract)\
                    .then_inc(x1lo_ready, 1)
                nc.vector.tensor_reduce(z0[:, bass.ds(SUPER * BLOCK_B * s, SUPER * BLOCK_B)],
                                        x1_bank[:, :].rearrange("p (b d) -> p b d", d=D), AX.X, ALU.add)\
                    .then_inc(z0_ready, 1)

            def mac_chunk(n, nb, i):
                c = DVE_CHUNKS[i]
                par, q = nb // SUPER, nb % SUPER
                wait(dve, t_ready, CHUNKS * n + c + 1)
                if i == 0:
                    wait(dve, fold_step, FOLDS * (n - 2) + 4)
                for x in range(CHUNK_J):
                    if i:
                        wait(dve, mac_done, MACS * n + CHUNK_J * (i - 1) + x + 1)
                    j = CHUNK_J * c + x
                    nc.vector.scalar_tensor_tensor(acc[nb % 2][:, x, :],
                                                   t_bank[(CHUNKS * nb + c) % T_BANKS][:, x * H:(x + 1) * H],
                                                   x_scale[par][:, q, j:j + 1],
                                                   acc[nb % 2][:, x, :] if i else acc_start[:, x, :],
                                                   ALU.mult, ALU.add).then_inc(mac_done, 1)

            def pair(p, first=False, last=False):
                for nb in range(PAIR_BLOCKS):
                    n, par, q = PAIR_BLOCKS * p + nb, nb // SUPER, nb % SUPER
                    s = 2 * p + par
                    tiles = [] if last and par else SLOT_TILES[q]
                    u0, upar = TILES * (s + 1), TILES * (1 - par)
                    s_next, q_next = (s, q + 1) if q < SUPER - 1 else (s + 1, 0)
                    par_next = par if q < SUPER - 1 else 1 - par
                    next_last = last and (par or q == SUPER - 1)
                    nxt = [] if next_last else SLOT_TILES[q_next]
                    if q == 0:
                        wait(dve, scale_loaded[par], 16 * (p + 1))

                    def make(i):
                        if i < len(nxt):
                            product(1 - par_next, nxt[i], TILES * (s_next + 1) + nxt[i], p + 2)

                    mac_chunk(n, nb, 0)
                    if tiles:
                        tile_lo(u0 + tiles[0], (upar + tiles[0]) % 2, tiles[0])
                    mac_chunk(n, nb, 1)
                    make(0)
                    mac_chunk(n, nb, 2)
                    if len(tiles) > 1:
                        tile_lo(u0 + tiles[1], (upar + tiles[1]) % 2, tiles[1])
                    if q == SUPER - 1 and tiles:
                        x1_low(s + 1, 1 - par)
                    mac_chunk(n, nb, 3)
                    make(1)
                    mac_chunk(n, nb, 4)
                    mac_chunk(n, nb, 5)

            dve.wait_ge(start_loaded, 16)
            product(0, 0, 0, 1)
            product(0, 1, 1, 1)
            for t in range(TILES):
                tile_lo(t, t % 2, t)
                if t + 2 < TILES:
                    product(0, t + 2, t + 2, 1)
                else:
                    product(1, t + 2 - TILES, t + 2, 1)
            x1_low(0, 0)
            pair(0, first=True)
            with dve.Fori(1, PAIRS - 1) as p:
                pair(p)
            pair(PAIRS - 1, last=True)

        @block.tensor
        def _(pe):
            def transpose_tile(u, par, t):
                wait(pe, prod_ready, u + 1)
                wait(pe, lo_ready, u - 1)
                k = TILE_R[t] * F
                for q in range(SUPER):
                    last = nc.tensor.transpose(pt_bank[par][0:k, q * P:(q + 1) * P], prod[par][:, q, 0:k], ident[:, :])
                last.then_inc(tr_ready, 1)

            def layer0_tile(u, par, t, s):
                wait(pe, lo_ready, u + 1)
                if t == 0:
                    wait(pe, z0_ready, s)
                k = TILE_R[t] * F
                terms = [(w0_hi, pt_hi), (w0_lo, pt_hi), (w0_hi, pt_lo)]
                for i, (w, x) in enumerate(terms):
                    last = nc.tensor.matmul(x1_bank[:, :], w[0:k, t, :], x[par][0:k, :],
                                            start=(t == 0 and i == 0), stop=(t == TILES - 1 and i == 2))
                last.then_inc(l0_done, 1)

            def layer1_chunk(n, nb, c):
                par, q = nb // SUPER, nb % SUPER
                k_local = CHUNKS * nb + c
                bank, w = t_bank[k_local % T_BANKS], chunk_fields(c) * H
                free, count = t_consumer((k_local - T_BANKS) % (CHUNKS * PAIR_BLOCKS))
                if k_local >= T_BANKS or not isinstance(n, int) or n >= PAIR_BLOCKS:
                    per_block = MACS if free == "dve" else len(ACT_CHUNKS)
                    base = (n - nb) * per_block - (0 if k_local >= T_BANKS else PAIR_BLOCKS * per_block)
                    wait(pe, mac_done if free == "dve" else scaled_ready, base + count)
                cols, rhs = slice(q * P, (q + 1) * P), slice(CHUNK_J * c * H, CHUNK_J * c * H + w)
                terms = [(x1_hi, w1_hi), (x1_hi, w1_lo), (x1_lo, w1_hi)]
                for i, (x, wt) in enumerate(terms):
                    last = nc.tensor.matmul(bank[:, 0:w], x[par][:, cols], wt[:, rhs], start=(i == 0), stop=(i == 2))
                last.then_inc(t_ready, 1)

            def form_g(m, mb, stored_z=None):
                par, q = mb // SUPER, mb % SUPER
                wait(pe, fold_step, FOLDS * (m + 1))
                wait(pe, g_stored, m)
                if stored_z is not None:
                    wait(pe, z2_stored, stored_z)
                nc.tensor.matmul(g_bank[:, 0:BD_W], x2[mb % 2][:, :], x_diag[par][:, q, :], start=True, stop=True)\
                    .then_inc(g_ready, 1)

            def pair(p, first=False, last=False, groups_done=None):
                for nb in range(PAIR_BLOCKS):
                    n, par, q = PAIR_BLOCKS * p + nb, nb // SUPER, nb % SUPER
                    s = 2 * p + par
                    tiles = [] if last and par else SLOT_TILES[q]
                    u0, upar = TILES * (s + 1), TILES * (1 - par)
                    if tiles:
                        transpose_tile(u0 + tiles[0], (upar + tiles[0]) % 2, tiles[0])
                    if q == 0:
                        wait(pe, x1lo_ready, s + 1)
                    layer1_chunk(n, nb, 0)
                    layer1_chunk(n, nb, 1)
                    if len(tiles) > 1:
                        transpose_tile(u0 + tiles[1], (upar + tiles[1]) % 2, tiles[1])
                    layer1_chunk(n, nb, 2)
                    layer1_chunk(n, nb, 3)
                    if tiles:
                        layer0_tile(u0 + tiles[0], (upar + tiles[0]) % 2, tiles[0], s + 1)
                    layer1_chunk(n, nb, 4)
                    if not (first and nb < LAG):
                        mb = (nb - LAG) % PAIR_BLOCKS
                        if q == LAG:
                            wait(pe, diag_loaded[par], 16 * BLOCK_B * (p + 1))
                        form_g(n - LAG, mb, groups_done if nb == 0 else None)
                    layer1_chunk(n, nb, 5)
                    if len(tiles) > 1:
                        layer0_tile(u0 + tiles[1], (upar + tiles[1]) % 2, tiles[1], s + 1)
                    for c in range(6, CHUNKS):
                        layer1_chunk(n, nb, c)

            def layer2(stored, width):
                wait(pe, g_stored, stored)
                for j in range(F):
                    last = nc.tensor.matmul(g_bank[:, 0:width], w2[:, j, :], g_all[:, 1 + j, 0:width],
                                            start=(j == 0), stop=(j == F - 1))
                last.then_inc(z2_ready, 1)

            pe.wait_ge(w_lo_ready, 5)
            pe.wait_ge(zeroed, 6)
            transpose_tile(0, 0, 0)
            for t in range(TILES):
                if t + 1 < TILES:
                    transpose_tile(t + 1, (t + 1) % 2, t + 1)
                layer0_tile(t, t % 2, t, 0)
            pe.wait_ge(w2_loaded, 16)
            pair(0, first=True)
            with pe.Fori(0, GROUPS - 1) as g:
                pair(2 * g + 1)
                layer2(GROUP_BLOCKS * (g + 1) - LAG, GROUP_B)
                pair(2 * g + 2, groups_done=g + 1)
            pair(PAIRS - 1, last=True)
            layer2(GROUP_BLOCKS * GROUPS - LAG, GROUP_B)
            for i in range(LAG):
                form_g(BLOCKS - LAG + i, PAIR_BLOCKS - LAG + i, GROUPS if i == 0 else None)
            layer2(BLOCKS, ZPAD)

            pe.wait_ge(top_loaded, 16 * 7)
            pe.wait_ge(z0_biased, 1)
            pe.wait_ge(z2_stored, GROUPS + 1)
            pe.wait_ge(z1_stored, GROUPS + 1)
            for i in range(8):
                half, m = divmod(i, 4)
                b = slice(half * BANK, (half + 1) * BANK)
                zb = slice(ZPAD + half * BANK, ZPAD + (half + 1) * BANK)
                operands = [(wt1[:, 0, :], z0[:, b]), (wt1[:, 1, :], z1[:, zb]), (wt1[:, 2, :], z2[:, zb]),
                            (wt1[0:D, 3, :], dense[:, b])]
                for x, (w, z) in enumerate(operands):
                    last = nc.tensor.matmul(mlp_bank(i)[:, :], w[:, m * P:(m + 1) * P], z, start=(x == 0), stop=(x == 3))
                last.then_inc(h1_ready, 1)
            for i in range(4):
                half, m = divmod(i, 2)
                b = slice(half * BANK, (half + 1) * BANK)
                pe.wait_ge(h1_stored, max(4 * (half + 1), i + 1))
                for x in range(4):
                    last = nc.tensor.matmul(mlp_bank(i)[:, :], wt2[:, x, m * P:(m + 1) * P], h1[:, x, b],
                                            start=(x == 0), stop=(x == 3))
                last.then_inc(h2_ready, 1)
            for half in range(2):
                pe.wait_ge(h2_stored, 2 * (half + 1))
                pe.wait_ge(h1_stored, 8)
                for x in range(2):
                    last = nc.tensor.matmul(mlp_bank(4 + half)[0:1, :], wt3[:, x:x + 1], h2[:, x, half * BANK:(half + 1) * BANK],
                                            start=(x == 0), stop=(x == 1))
            last.then_inc(y_ready, 1)


def kernel(**inputs):
    import numpy as np
    import concourse.bacc as bacc
    from concourse.bass_utils import run_bass_kernel_spmd

    n_tables = F
    w0 = np.asarray(inputs["L0_rec_W0"]).reshape(H, F, F)
    w0_a = np.zeros((P, TILES, H), w0.dtype)
    w0_b = np.zeros((P, TILES, H), w0.dtype)
    for r in range(RS):
        t, first = r // R_TILE, r % R_TILE * F
        j = np.arange(F)
        w0_a[first:first + F, t] = w0[:, j, (j + r) % F].T
        if r:
            w0_b[first:first + F, t] = w0[:, (j + r) % F, j].T

    def by_k(w):
        return np.ascontiguousarray(np.asarray(w).reshape(H, F, H).transpose(2, 1, 0)).reshape(P, F * H)

    def by_partition(v):
        return np.ascontiguousarray(np.asarray(v).reshape(-1, P).T)

    host = {
        "dense_t": np.ascontiguousarray(np.asarray(inputs["dense_ctx"]).T),
        "ids": np.ascontiguousarray(inputs["ids"]),
        "w_top1": np.asarray(inputs["W_top1"]), "b_top1": by_partition(inputs["b_top1"]),
        "w_top2": np.asarray(inputs["W_top2"]), "b_top2": by_partition(inputs["b_top2"]),
        "w_top3": by_partition(inputs["W_top3"]),
        "w0_a": w0_a.reshape(P, TILES * H), "w0_b": w0_b.reshape(P, TILES * H),
        "b0": np.asarray(inputs["L0_rec_b0"]).reshape(H, 1),
        "w1_t": by_k(inputs["L0_rec_W1"]), "b1": np.asarray(inputs["L0_rec_b1"]),
        "w2_t": by_k(inputs["L0_rec_W2"]), "b2": np.asarray(inputs["L0_rec_b2"]).reshape(H, 1),
    }
    tables = {f"tbl_{i}": np.asarray(inputs[f"tbl_{i}"]) for i in range(n_tables)}

    nc = bacc.Bacc("TRN2", target_bir_lowering=False, num_devices=1)

    def external(name, a):
        return nc.dram_tensor(name, a.shape, mybir.dt.from_np(a.dtype), kind="ExternalInput").ap()

    args = {name: external(name, a) for name, a in host.items()}
    table_args = [external(name, a) for name, a in tables.items()]
    out = nc.dram_tensor("out", (1, B), mybir.dt.float32, kind="ExternalOutput").ap()
    dlrm_cin_tower(nc, tables=table_args, out=out, **args)
    result = run_bass_kernel_spmd(nc, [{**host, **tables}], core_ids=[0])
    return result.results[0]["out"].reshape(B, 1)
```

```python
from contextlib import ExitStack

import concourse.bass as bass
from concourse import mybir

B, F, D, H = 1024, 39, 16, 128
P = 128
BLOCK_B = P // D
BLOCKS = B // BLOCK_B
SUPER = 4
SUPERS = BLOCKS // SUPER
PAIRS = SUPERS // 2
PAIR_BLOCKS = 2 * SUPER
GROUP_B = 128
GROUPS = B // GROUP_B
GROUP_BLOCKS = GROUP_B // BLOCK_B
LAG = 2
BANK = 512

RS = (F + 1) // 2
R_TILE = 3
TILES = -(-RS // R_TILE)
TILE_R = [min(R_TILE, RS - R_TILE * t) for t in range(TILES)]
SLOT_TILES = [[0, 1], [2, 3], [4, 5], [6]]

CHUNK_J = 4
CHUNKS = -(-F // CHUNK_J)
T_BANKS = 4
DVE_CHUNKS = [0, 2, 4, 6, 8, 9]
ACT_CHUNKS = [1, 3, 5, 7]
MACS = F - CHUNK_J * len(ACT_CHUNKS)
PT_BANKS = 2
CHAINS = 2
FOLDS = 6
FOLD_READ = [1, 1, 2, 3]

SUPER_B = SUPER * BLOCK_B
QUARTERS = P // SUPER_B
GATHERS = -(-F // QUARTERS)
ROW = QUARTERS * GATHERS
ROWS_AT = 1
LEAD = 3

EXT = F + RS - 1
GC = F + 1
BD_W = BLOCK_B * GC

H1, H2 = 512, 256
ZPAD = LAG * BLOCK_B

PE_SLOT = [("transpose", 0), ("chunk", 0), ("chunk", 1), ("chunk", 2), ("chunk", 3), ("transpose", 1),
           ("chunk", 4), ("multiply", 0), ("chunk", 5), ("g", 0), ("chunk", 6), ("chunk", 7),
           ("multiply", 1), ("chunk", 8), ("chunk", 9)]
DVE_SLOT = [("chunk", 0), ("low", 0), ("chunk", 1), ("product", 0), ("low", 1), ("chunk", 2), ("x1", 0),
            ("chunk", 3), ("product", 1), ("chunk", 4), ("chunk", 5)]
ACT_SLOT = [("high", 0), ("chunk", 0), ("chunk", 1), ("high", 1), ("x1", 0), ("g", 0), ("chunk", 2), ("chunk", 3)]


def chunk_fields(c):
    return min(CHUNK_J, F - CHUNK_J * c)


def wait(engine, semaphore, value):
    if isinstance(value, int) and value <= 0:
        return
    engine.wait_ge(semaphore, value)


def t_consumer(k_local):
    n, c = divmod(k_local, CHUNKS)
    if c in DVE_CHUNKS:
        return "dve", MACS * n + sum(chunk_fields(d) for d in DVE_CHUNKS if d <= c)
    return "act", len(ACT_CHUNKS) * n + ACT_CHUNKS.index(c) + 1


def dlrm_cin_tower(nc, dense_t, ids, table_starts, table, w_top1, b_top1, w_top2, b_top2, w_top3,
                   w0_a, w0_b, b0, w1_t, b1, w2_t, b2, out):
    f32, f32r, i32 = mybir.dt.float32, mybir.dt.float32r, mybir.dt.int32
    ALU, ACT = mybir.AluOpType, mybir.ActivationFunctionType
    AX = mybir.AxisListType

    rows_dram = nc.dram_tensor("x0_rows", (B * D, ROW), f32)[:, :]
    rows_by_block = rows_dram.rearrange("(n p) c -> p n c", p=P)
    rows_by_super = rows_dram.rearrange("(s b d) c -> b s d c", b=SUPER_B, d=D)

    ctx = ExitStack()
    with ctx:
        def sb(name, shape, dt=f32):
            return ctx.enter_context(nc.sbuf_tensor(name, shape, dt))

        def sem(name):
            return ctx.enter_context(nc.semaphore(name))

        w1_hi, w1_lo = sb("w1_hi", [P, F * H], f32r), sb("w1_lo", [P, F * H], f32r)
        w2 = sb("w2", [P, F, H])
        w0_hi, w0_lo = sb("w0_hi", [P, TILES, H], f32r), sb("w0_lo", [P, TILES, H], f32r)
        wt1 = sb("wt1", [P, 4, H1])
        wt2 = sb("wt2", [P, 4, H2])
        wt3 = sb("wt3", [P, 2])
        bt1, bt2 = sb("bt1", [P, 4]), sb("bt2", [P, 2])
        b_cin = sb("b_cin", [P, 2])
        b_cin16 = sb("b_cin16", [P, 2])
        acc_start = sb("acc_start", [P, CHAINS, H])
        dense = sb("dense", [D, B])
        ident = sb("ident", [P, P])
        ids_all = sb("ids_all", [P, SUPERS, GATHERS], i32)
        starts = sb("starts", [P, GATHERS], i32)
        idx_all = sb("idx_all", [P, SUPERS + 1, GATHERS], i32)
        idx = [sb(f"idx{i}", [P, GATHERS], i32) for i in range(2)]
        emb = [sb(f"emb{i}", [P, GATHERS, D]) for i in range(2)]
        rows = [sb(f"rows{i}", [P, D, GATHERS]) for i in range(2)]
        x_pairs = [sb(f"x_pairs{i}", [P, SUPER, EXT]) for i in range(2)]
        x_scale = [sb(f"x_scale{i}", [P, SUPER, F]) for i in range(2)]
        x_diag = [sb(f"x_diag{i}", [P, SUPER, BD_W]) for i in range(2)]
        prod = [sb(f"prod{i}", [P, SUPER, R_TILE * F]) for i in range(2)]
        pt_hi = [sb(f"pt_hi{i}", [P, BANK], f32r) for i in range(2)]
        pt_lo = [sb(f"pt_lo{i}", [P, BANK], f32r) for i in range(2)]
        x1_hi = [sb(f"x1_hi{i}", [P, BANK], f32r) for i in range(2)]
        x1_lo = [sb(f"x1_lo{i}", [P, BANK], f32r) for i in range(2)]
        acc = [sb(f"acc{i}", [P, CHAINS, H]) for i in range(2)]
        scaled = [sb(f"scaled{i}", [P, CHUNK_J * H]) for i in range(len(ACT_CHUNKS))]
        fold = sb("fold", [P, CHUNK_J * H])
        x2 = [sb(f"x2_{i}", [P, H]) for i in range(2)]
        g_all = sb("g_all", [P, GC, GROUP_B])
        z0 = sb("z0", [P, B])
        z1, z2 = sb("z1", [P, ZPAD + B]), sb("z2", [P, ZPAD + B])
        h1 = sb("h1", [P, 4, B])
        h2 = sb("h2", [P, 2, B])
        y = sb("y", [1, B])
        W1_PART = F * H // 4
        w1_stage = [h1[:, :, :].rearrange("p a b -> p (a b)")[:, i * W1_PART:(i + 1) * W1_PART]
                    for i in range(3)] + [h2[:, :, :].rearrange("p a b -> p (a b)")[:, 0:W1_PART]]
        w0_stage_a, w0_stage_b = z1[:, 0:TILES * H], z2[:, 0:TILES * H]
        w0_sum = z0[:, 0:TILES * H]

        t_bank = [ctx.enter_context(nc.psum_tensor(f"t_bank{i}", [P, BANK], f32)) for i in range(T_BANKS)]
        pt_banks = [ctx.enter_context(nc.psum_tensor(f"pt_bank{i}", [P, BANK], f32)) for i in range(PT_BANKS)]
        x1_bank = ctx.enter_context(nc.psum_tensor("x1_bank", [P, BANK], f32))
        g_bank = ctx.enter_context(nc.psum_tensor("g_bank", [P, BANK], f32))

        ids_loaded, w0_loaded = sem("ids_loaded"), sem("w0_loaded")
        w1_loaded = sem("w1_loaded")
        bias_loaded, start_loaded = sem("bias_loaded"), sem("start_loaded")
        w2_loaded, top_loaded = sem("w2_loaded"), sem("top_loaded")
        diag_made = sem("diag_made")
        zeroed = sem("zeroed")
        idx_ready = sem("idx_ready")
        idx_all_ready = sem("idx_all_ready")
        gathered = [sem("gathered0"), sem("gathered1")]
        rows_made = sem("rows_made")
        rows_stored = [sem("rows_stored0"), sem("rows_stored1")]
        pairs_loaded = [sem("pairs_loaded0"), sem("pairs_loaded1")]
        scale_loaded = [sem("scale_loaded0"), sem("scale_loaded1")]
        diag_loaded = [sem("diag_loaded0"), sem("diag_loaded1")]
        b16_ready = sem("b16_ready")
        w0_summed, w_hi_ready, w_lo_ready = sem("w0_summed"), sem("w_hi_ready"), sem("w_lo_ready")
        prod_ready, tr_ready = sem("prod_ready"), sem("tr_ready")
        hi_ready, lo_ready = sem("hi_ready"), sem("lo_ready")
        l0_done = sem("l0_done")
        x1hi_ready, x1lo_ready, z0_ready = sem("x1hi_ready"), sem("x1lo_ready"), sem("z0_ready")
        t_ready = sem("t_ready")
        mac_done = sem("mac_done")
        scaled_ready = sem("scaled_ready")
        fold_step = sem("fold_step")
        g_ready, g_stored = sem("g_ready"), sem("g_stored")
        z1_stored = sem("z1_stored")
        z2_ready, z2_stored = sem("z2_ready"), sem("z2_stored")
        z0_biased = sem("z0_biased")
        h1_ready, h1_stored = sem("h1_ready"), sem("h1_stored")
        h2_ready, h2_stored = sem("h2_ready"), sem("h2_stored")
        y_ready, y_stored, y_written = sem("y_ready"), sem("y_stored"), sem("y_written")

        block = ctx.enter_context(nc.Block())

        def mlp_bank(i):
            return (t_bank + pt_banks + [x1_bank, g_bank])[i]

        def x_window(buf, t):
            base = buf[:, :, R_TILE * t:R_TILE * t + F]
            (ps, pn), (bs, bn), (js, jn) = base.ap
            return bass.AP(tensor=base.tensor, offset=base.offset,
                           ap=[[ps, pn], [bs, bn], [1, TILE_R[t]], [js, jn]])

        STORE = 16 * QUARTERS
        GATHERED = 16 * GATHERS

        @block.sync
        def _(sp):
            sp.dma_start(ids_all[:, :, :].rearrange("p s f -> p (s f)"), ids).then_inc(ids_loaded, 16)
            sp.dma_start(starts[:, :], table_starts).then_inc(ids_loaded, 16)
            sp.dma_start(w0_stage_a, w0_a).then_inc(w0_loaded, 16)
            sp.dma_start(w0_stage_b, w0_b).then_inc(w0_loaded, 16)
            sp.dma_start(b_cin[:, 0:1], b0).then_inc(bias_loaded, 16)
            sp.dma_start(b_cin[:, 1:2], b2).then_inc(bias_loaded, 16)
            for i in range(4):
                sp.dma_start(w1_stage[i], w1_t[:, i * W1_PART:(i + 1) * W1_PART]).then_inc(w1_loaded, 16)
            sp.wait_ge(zeroed, 1)
            sp.dma_start(acc_start[:, 0, :], b1.partition_broadcast(P)).then_inc(start_loaded, 16)
            sp.dma_start(w2[:, :, :].rearrange("p j h -> p (j h)"), w2_t).then_inc(w2_loaded, 16)

            def load_pairs(s, par):
                for first, n in ((0, F), (F, EXT - F)):
                    sp.dma_start(x_pairs[par][:, :, first:first + n], rows_by_block[:, bass.ds(SUPER * s, SUPER), 0:n])\
                      .then_inc(pairs_loaded[par], 16)

            def load_scale(s, par):
                sp.dma_start(x_scale[par][:, :, :], rows_by_block[:, bass.ds(SUPER * s, SUPER), 0:F])\
                  .then_inc(scale_loaded[par], 16)

            def load_diag(s, par):
                for i in reversed(range(BLOCK_B)):
                    r = slice(D * i, D * (i + 1))
                    sp.dma_start(x_diag[par][r, :, GC * i + 1:GC * (i + 1)],
                                 rows_by_block[r, bass.ds(SUPER * s, SUPER), 0:F])\
                      .then_inc(diag_loaded[par], 16)

            def step(s, par, last):
                wait(sp, g_ready, SUPER * s)
                load_diag(s + 1, 1 - par)
                if last:
                    return
                wait(sp, prod_ready, TILES * (s + 1))
                wait(sp, rows_stored[par], STORE * (s // 2 + 2))
                load_pairs(s + 2, par)
                wait(sp, fold_step, FOLDS * SUPER * (s + 1))
                load_scale(s + 2, par)

            sp.wait_ge(rows_stored[0], STORE)
            sp.wait_ge(diag_made, 8)
            load_pairs(0, 0)
            load_scale(0, 0)
            load_diag(0, 0)
            sp.wait_ge(rows_stored[1], STORE)
            load_pairs(1, 1)
            load_scale(1, 1)
            step(0, 0, False)
            step(1, 1, False)
            sp.dma_start(wt1[:, 0:3, :], w_top1[0:3 * P, :].rearrange("(t p) n -> p t n", p=P)).then_inc(top_loaded, 16)
            sp.dma_start(wt1[0:D, 3, :], w_top1[3 * P:3 * P + D, :]).then_inc(top_loaded, 16)
            sp.dma_start(wt2[:, :, :], w_top2.rearrange("(t p) n -> p t n", p=P)).then_inc(top_loaded, 16)
            sp.dma_start(wt3[:, :], w_top3).then_inc(top_loaded, 16)
            sp.dma_start(bt1[:, :], b_top1).then_inc(top_loaded, 16)
            sp.dma_start(bt2[:, :], b_top2).then_inc(top_loaded, 16)
            sp.dma_start(dense[:, :], dense_t).then_inc(top_loaded, 16)
            with sp.Fori(1, PAIRS - 1) as p:
                for par in range(2):
                    s = 2 * p + par
                    wait(sp, g_ready, SUPER * s)
                    load_diag(s + 1, 1 - par)
                    wait(sp, prod_ready, TILES * (s + 1))
                    wait(sp, rows_stored[par], STORE * (p + 2))
                    load_pairs(s + 2, par)
                    wait(sp, fold_step, FOLDS * SUPER * (s + 1))
                    load_scale(s + 2, par)
            step(SUPERS - 2, 0, True)
            sp.wait_ge(y_stored, 1)
            sp.dma_start(out, y[:, :]).then_inc(y_written, 16)
            sp.wait_ge(y_written, 16)

        @block.gpsimd
        def _(pool):
            pool.memset(acc_start[:, :, :], 0.0).then_inc(zeroed, 1)
            pool.memset(idx_all[:, SUPERS, :], 0).then_inc(zeroed, 1)
            pool.wait_ge(ids_loaded, 32)
            pool.tensor_tensor(idx_all[:, 0:SUPERS, :], ids_all[:, :, :],
                               starts[:, :].unsqueeze(1).to_broadcast([P, SUPERS, GATHERS]),
                               ALU.add).then_inc(idx_all_ready, 1)
            pool.wait_ge(idx_all_ready, 1)

            def take_idx(s, par):
                wait(pool, rows_made, s - 1)
                pool.tensor_copy(idx[par][:, :], idx_all[:, bass.ds(s, 1), :].rearrange("p g f -> p (g f)"))\
                    .then_inc(idx_ready, 1)
                wait(pool, idx_ready, s + 1)

            def gather(par, i):
                pool.indirect_dma_start(out=emb[par][:, i, :], out_offset=None, in_=table,
                                        in_offset=bass.IndirectOffsetOnAxis(ap=idx[par][:, i:i + 1], axis=0))\
                    .then_inc(gathered[par], 16)

            take_idx(0, 0)
            for i in range(GATHERS):
                gather(0, i)
            take_idx(1, 1)
            for i in range(GATHERS):
                gather(1, i)
            for n, x in enumerate(x_diag):
                pool.memset(x[:, :, :], 0.0).then_inc(diag_made, 1)
                wait(pool, diag_made, 4 * n + 1)
                ones = x[:, :, :].rearrange("p q (b c) -> p q b c", c=GC)[:, :, :, 0]
                pool.memset(ones, 1.0).then_inc(diag_made, 1)
                wait(pool, diag_made, 4 * n + 2)
                pool.affine_select(out=ones, in_=ones, compare_op=ALU.is_ge, fill=0.0, base=0,
                                   pattern=[[0, SUPER], [-D, BLOCK_B]], channel_multiplier=1).then_inc(diag_made, 1)
                wait(pool, diag_made, 4 * n + 3)
                pool.affine_select(out=ones, in_=ones, compare_op=ALU.is_ge, fill=0.0, base=D - 1,
                                   pattern=[[0, SUPER], [D, BLOCK_B]], channel_multiplier=-1).then_inc(diag_made, 1)
            pool.memset(ident[:, :], 0.0).then_inc(zeroed, 1)
            pool.wait_ge(zeroed, 3)
            pool.affine_select(out=ident[:, :], in_=ident[:, :], compare_op=ALU.not_equal, fill=1.0,
                               base=0, pattern=[[-1, P]], channel_multiplier=1).then_inc(zeroed, 1)
            pool.memset(g_all[:, :, 0:ZPAD], 0.0).then_inc(zeroed, 1)
            take_idx(2, 0)
            for i in range(GATHERS):
                gather(0, i)

            def folds(n, nb):
                a = acc[nb % 2][:, :, :].rearrange("p c h -> p (c h)")
                s1, s2 = CHUNK_J * H // 2, CHUNK_J * H // 4
                wait(pool, scaled_ready, 4 * n + 2)
                wait(pool, fold_step, FOLDS * n)
                pool.tensor_tensor(fold[:, :], scaled[0][:, :], scaled[1][:, :], ALU.add).then_inc(fold_step, 1)
                wait(pool, scaled_ready, 4 * n + 3)
                wait(pool, fold_step, FOLDS * n + 1)
                pool.tensor_tensor(fold[:, :], fold[:, :], scaled[2][:, :], ALU.add).then_inc(fold_step, 1)
                wait(pool, scaled_ready, 4 * n + 4)
                wait(pool, fold_step, FOLDS * n + 2)
                pool.tensor_tensor(fold[:, :], fold[:, :], scaled[3][:, :], ALU.add).then_inc(fold_step, 1)
                wait(pool, fold_step, FOLDS * n + 3)
                pool.tensor_tensor(fold[:, 0:s1], fold[:, 0:s1], fold[:, s1:2 * s1], ALU.add).then_inc(fold_step, 1)
                wait(pool, mac_done, MACS * (n + 1))
                wait(pool, fold_step, FOLDS * n + 4)
                pool.tensor_tensor(fold[:, 0:s1], fold[:, 0:s1], a, ALU.add).then_inc(fold_step, 1)
                wait(pool, fold_step, FOLDS * n + 5)
                wait(pool, g_ready, n - 1)
                pool.tensor_tensor(x2[nb % 2][:, :], fold[:, 0:s2], fold[:, s2:2 * s2], ALU.add).then_inc(fold_step, 1)

            def pair(p, last=False):
                for nb in range(PAIR_BLOCKS):
                    par, q = nb // SUPER, nb % SUPER
                    to = (par + LEAD) % 2
                    if q == 0 and not last:
                        take_idx(2 * p + par + LEAD, to)
                    folds(PAIR_BLOCKS * p + nb, nb)
                    if not last:
                        for i in range(GATHERS * q // SUPER, GATHERS * (q + 1) // SUPER):
                            gather(to, i)

            pair(0)
            with pool.Fori(1, PAIRS - 1) as p:
                pair(p)
            pair(PAIRS - 1, last=True)
            pool.wait_ge(gathered[0], GATHERED * (PAIRS + 1))
            pool.wait_ge(gathered[1], GATHERED * PAIRS)

        @block.scalar
        def _(act):
            def store_rows(s, par, turn):
                wait(act, gathered[par], GATHERED * (turn + 1))
                wait(act, rows_stored[par], STORE * turn)
                nc.scalar.copy(rows[par][:, :, :], emb[par][:, :, :].rearrange("p f d -> p d f"))\
                    .then_inc(rows_made, 1)
                wait(act, rows_made, s + 1)
                for i in range(QUARTERS):
                    act.dma_start(rows_by_super[:, bass.ds(s, 1), :, GATHERS * i:GATHERS * (i + 1)],
                                  rows[par][SUPER_B * i:SUPER_B * (i + 1), :, :]
                                  .rearrange("p (o d) c -> p o d c", o=1)).then_inc(rows_stored[par], 16)

            act.wait_ge(w0_summed, 1)
            nc.scalar.copy(w0_hi[:, :, :].rearrange("p t h -> p (t h)"), w0_sum).then_inc(w_hi_ready, 1)
            store_rows(0, 0, 0)
            act.wait_ge(w1_loaded, 64)
            for i in range(4):
                nc.scalar.copy(w1_hi[:, i * W1_PART:(i + 1) * W1_PART], w1_stage[i]).then_inc(w_hi_ready, 1)

            def tile_hi(u, par, t):
                wait(act, tr_ready, u + 1)
                wait(act, l0_done, u - 1)
                k = TILE_R[t] * F
                nc.scalar.copy(pt_hi[par][0:k, :], pt_banks[par % PT_BANKS][0:k, :]).then_inc(hi_ready, 1)

            def x1_high(s, par):
                wait(act, l0_done, TILES * (s + 1))
                wait(act, t_ready, CHUNKS * SUPER * (s - 1))
                nc.scalar.activation(x1_hi[par][:, :], x1_bank[:, :], ACT.Identity, bias=b_cin[:, 0:1])\
                    .then_inc(x1hi_ready, 1)

            def scale_chunk(n, nb, a):
                c = ACT_CHUNKS[a]
                par, q = nb // SUPER, nb % SUPER
                wait(act, t_ready, CHUNKS * n + c + 1)
                wait(act, fold_step, FOLDS * (n - 1) + FOLD_READ[a])
                for i in range(chunk_fields(c)):
                    j = CHUNK_J * c + i
                    last = nc.scalar.activation(scaled[a][:, i * H:(i + 1) * H],
                                                t_bank[(CHUNKS * nb + c) % T_BANKS][:, i * H:(i + 1) * H],
                                                ACT.Copy, scale=x_scale[par][:, q, j:j + 1])
                last.then_inc(scaled_ready, 1)

            def store_g(m, slot):
                wait(act, g_ready, m + 1)
                nc.scalar.copy(g_all[:, :, BLOCK_B * slot:BLOCK_B * (slot + 1)],
                               g_bank[:, 0:BD_W].rearrange("p (b c) -> p c b", c=GC)).then_inc(g_stored, 1)

            def pair(p, half, first=False, last=False):
                for nb in range(PAIR_BLOCKS):
                    n, par, q = PAIR_BLOCKS * p + nb, nb // SUPER, nb % SUPER
                    s = 2 * p + par
                    tiles = [] if last and par else SLOT_TILES[q]
                    u0 = TILES * (s + 1)
                    if q == 0:
                        wait(act, scale_loaded[par], 16 * (p + 1))
                    if q == ROWS_AT and not last:
                        store_rows(s + 2, par, p + 1)
                    for what, i in ACT_SLOT:
                        if what == "chunk":
                            scale_chunk(n, nb, i)
                        elif what == "high" and i < len(tiles):
                            tile_hi(u0 + tiles[i], (TILES * (1 - par) + tiles[i]) % 2, tiles[i])
                        elif what == "x1" and q == SUPER - 1 and tiles:
                            x1_high(s + 1, 1 - par)
                        elif what == "g" and not (first and nb < LAG):
                            store_g(n - LAG, PAIR_BLOCKS * half + nb)

            def store_z(g, lo, width, stored):
                wait(act, g_stored, stored)
                nc.scalar.copy(z1[:, bass.ds(lo, width)], g_all[:, 0, 0:width]).then_inc(z1_stored, 1)
                wait(act, z2_ready, g + 1)
                nc.scalar.activation(z2[:, bass.ds(lo, width)], g_bank[:, 0:width], ACT.Identity,
                                     bias=b_cin16[:, 1:2]).then_inc(z2_stored, 1)

            act.wait_ge(bias_loaded, 32)
            act.wait_ge(w_lo_ready, 5)
            for t in range(TILES):
                tile_hi(t, t % 2, t)
                if t == 3:
                    store_rows(1, 1, 0)
            x1_high(0, 0)
            act.wait_ge(zeroed, 5)
            act.wait_ge(b16_ready, 1)
            pair(0, 0, first=True)
            with act.Fori(0, GROUPS - 1) as g:
                pair(2 * g + 1, 1)
                store_z(g, GROUP_B * g, GROUP_B, GROUP_BLOCKS * (g + 1) - LAG)
                pair(2 * g + 2, 0)
            pair(PAIRS - 1, 1, last=True)
            store_z(GROUPS - 1, GROUP_B * (GROUPS - 1), GROUP_B, GROUP_BLOCKS * GROUPS - LAG)
            for i in range(LAG):
                store_g(BLOCKS - LAG + i, i)
            store_z(GROUPS, B, ZPAD, BLOCKS)
            act.wait_ge(z0_ready, SUPERS)
            nc.scalar.activation(z0[:, :], z0[:, :], ACT.Identity, bias=b_cin16[:, 0:1]).then_inc(z0_biased, 1)
            act.wait_ge(top_loaded, 16 * 7)
            for i in range(8):
                half, m = divmod(i, 4)
                act.wait_ge(h1_ready, i + 1)
                nc.scalar.activation(h1[:, m, half * BANK:(half + 1) * BANK], mlp_bank(i)[:, :], ACT.Relu,
                                     bias=bt1[:, m:m + 1]).then_inc(h1_stored, 1)
            for i in range(4):
                half, m = divmod(i, 2)
                act.wait_ge(h2_ready, i + 1)
                nc.scalar.activation(h2[:, m, half * BANK:(half + 1) * BANK], mlp_bank(i)[:, :], ACT.Relu,
                                     bias=bt2[:, m:m + 1]).then_inc(h2_stored, 1)
            act.wait_ge(y_ready, 1)
            nc.scalar.copy(y[:, 0:BANK], mlp_bank(4)[0:1, :])
            nc.scalar.copy(y[:, BANK:B], mlp_bank(5)[0:1, :]).then_inc(y_stored, 1)
            for stored in rows_stored:
                act.wait_ge(stored, STORE * PAIRS)

        @block.vector
        def _(dve):
            dve.wait_ge(bias_loaded, 32)
            nc.vector.tensor_scalar(b_cin16[:, :], b_cin[:, :], float(D), None, ALU.mult).then_inc(b16_ready, 1)
            dve.wait_ge(w0_loaded, 32)
            nc.vector.tensor_tensor(w0_sum, w0_stage_a, w0_stage_b, ALU.add).then_inc(w0_summed, 1)
            dve.wait_ge(w0_summed, 1)
            dve.wait_ge(w_hi_ready, 1)
            nc.vector.tensor_tensor(w0_lo[:, :, :].rearrange("p t h -> p (t h)"), w0_sum,
                                    w0_hi[:, :, :].rearrange("p t h -> p (t h)").bitcast(f32),
                                    ALU.subtract).then_inc(w_lo_ready, 1)
            for i in range(4):
                part = slice(i * W1_PART, (i + 1) * W1_PART)
                dve.wait_ge(w_hi_ready, i + 2)
                nc.vector.tensor_tensor(w1_lo[:, part], w1_stage[i], w1_hi[:, part].bitcast(f32),
                                        ALU.subtract).then_inc(w_lo_ready, 1)

            def product(par, t, u, loads):
                if t == 0:
                    wait(dve, pairs_loaded[par], 32 * loads)
                wait(dve, tr_ready, u - 1)
                r = TILE_R[t]
                a = x_pairs[par][:, :, 0:F].unsqueeze(2).to_broadcast([P, SUPER, r, F])
                upar = (TILES * par + t) % 2
                nc.vector.tensor_tensor(prod[upar][:, :, 0:r * F].rearrange("p q (r j) -> p q r j", r=r),
                                        a, x_window(x_pairs[par], t), ALU.mult).then_inc(prod_ready, 1)

            def tile_lo(u, par, t):
                wait(dve, hi_ready, u + 1)
                wait(dve, l0_done, u - 1)
                k = TILE_R[t] * F
                nc.vector.tensor_tensor(pt_lo[par][0:k, :], pt_banks[par % PT_BANKS][0:k, :], pt_hi[par][0:k, :].bitcast(f32),
                                        ALU.subtract).then_inc(lo_ready, 1)

            def x1_low(s, par):
                wait(dve, x1hi_ready, s + 1)
                nc.vector.scalar_tensor_tensor(x1_lo[par][:, :], x1_bank[:, :], b_cin[:, 0:1],
                                               x1_hi[par][:, :].bitcast(f32), ALU.add, ALU.subtract)\
                    .then_inc(x1lo_ready, 1)
                nc.vector.tensor_reduce(z0[:, bass.ds(SUPER * BLOCK_B * s, SUPER * BLOCK_B)],
                                        x1_bank[:, :].rearrange("p (b d) -> p b d", d=D), AX.X, ALU.add)\
                    .then_inc(z0_ready, 1)

            def mac_chunk(n, nb, i):
                c = DVE_CHUNKS[i]
                par, q = nb // SUPER, nb % SUPER
                wait(dve, t_ready, CHUNKS * n + c + 1)
                if i == 0:
                    wait(dve, fold_step, FOLDS * (n - 2) + 5)
                for x in range(chunk_fields(c)):
                    e, chain = CHUNK_J * i + x, x % CHAINS
                    if e >= CHAINS:
                        wait(dve, mac_done, MACS * n + e - CHAINS + 1)
                    j = CHUNK_J * c + x
                    nc.vector.scalar_tensor_tensor(acc[nb % 2][:, chain, :],
                                                   t_bank[(CHUNKS * nb + c) % T_BANKS][:, x * H:(x + 1) * H],
                                                   x_scale[par][:, q, j:j + 1],
                                                   acc[nb % 2][:, chain, :] if e >= CHAINS else acc_start[:, chain, :],
                                                   ALU.mult, ALU.add).then_inc(mac_done, 1)

            def pair(p, first=False, last=False):
                for nb in range(PAIR_BLOCKS):
                    n, par, q = PAIR_BLOCKS * p + nb, nb // SUPER, nb % SUPER
                    s = 2 * p + par
                    tiles = [] if last and par else SLOT_TILES[q]
                    u0, upar = TILES * (s + 1), TILES * (1 - par)
                    s_next, q_next = (s, q + 1) if q < SUPER - 1 else (s + 1, 0)
                    par_next = par if q < SUPER - 1 else 1 - par
                    next_last = last and (par or q == SUPER - 1)
                    nxt = [] if next_last else SLOT_TILES[q_next]
                    if q == 0:
                        wait(dve, scale_loaded[par], 16 * (p + 1))

                    for what, i in DVE_SLOT:
                        if what == "chunk":
                            mac_chunk(n, nb, i)
                        elif what == "low" and i < len(tiles):
                            tile_lo(u0 + tiles[i], (upar + tiles[i]) % 2, tiles[i])
                        elif what == "x1" and q == SUPER - 1 and tiles:
                            x1_low(s + 1, 1 - par)
                        elif what == "product" and i < len(nxt):
                            product(1 - par_next, nxt[i], TILES * (s_next + 1) + nxt[i], p + 2)

            dve.wait_ge(start_loaded, 16)
            product(0, 0, 0, 1)
            product(0, 1, 1, 1)
            for t in range(TILES):
                tile_lo(t, t % 2, t)
                if t + 2 < TILES:
                    product(0, t + 2, t + 2, 1)
                else:
                    product(1, t + 2 - TILES, t + 2, 1)
            x1_low(0, 0)
            pair(0, first=True)
            with dve.Fori(1, PAIRS - 1) as p:
                pair(p)
            pair(PAIRS - 1, last=True)

        @block.tensor
        def _(pe):
            def transpose_tile(u, par, t):
                wait(pe, prod_ready, u + 1)
                wait(pe, lo_ready, u + 1 - PT_BANKS)
                k = TILE_R[t] * F
                for q in range(SUPER):
                    last = nc.tensor.transpose(pt_banks[par % PT_BANKS][0:k, q * P:(q + 1) * P], prod[par][:, q, 0:k], ident[:, :])
                last.then_inc(tr_ready, 1)

            def layer0_tile(u, par, t, s):
                wait(pe, lo_ready, u + 1)
                if t == 0:
                    wait(pe, z0_ready, s)
                k = TILE_R[t] * F
                terms = [(w0_hi, pt_hi), (w0_lo, pt_hi), (w0_hi, pt_lo)]
                for i, (w, x) in enumerate(terms):
                    last = nc.tensor.matmul(x1_bank[:, :], w[0:k, t, :], x[par][0:k, :],
                                            start=(t == 0 and i == 0), stop=(t == TILES - 1 and i == 2))
                last.then_inc(l0_done, 1)

            def layer1_chunk(n, nb, c):
                par, q = nb // SUPER, nb % SUPER
                k_local = CHUNKS * nb + c
                bank, w = t_bank[k_local % T_BANKS], chunk_fields(c) * H
                free, count = t_consumer((k_local - T_BANKS) % (CHUNKS * PAIR_BLOCKS))
                if k_local >= T_BANKS or not isinstance(n, int) or n >= PAIR_BLOCKS:
                    per_block = MACS if free == "dve" else len(ACT_CHUNKS)
                    base = (n - nb) * per_block - (0 if k_local >= T_BANKS else PAIR_BLOCKS * per_block)
                    wait(pe, mac_done if free == "dve" else scaled_ready, base + count)
                cols, rhs = slice(q * P, (q + 1) * P), slice(CHUNK_J * c * H, CHUNK_J * c * H + w)
                terms = [(x1_hi, w1_hi), (x1_hi, w1_lo), (x1_lo, w1_hi)]
                for i, (x, wt) in enumerate(terms):
                    last = nc.tensor.matmul(bank[:, 0:w], x[par][:, cols], wt[:, rhs], start=(i == 0), stop=(i == 2))
                last.then_inc(t_ready, 1)

            def form_g(m, mb, stored_z=None):
                par, q = mb // SUPER, mb % SUPER
                wait(pe, fold_step, FOLDS * (m + 1))
                wait(pe, g_stored, m)
                if stored_z is not None:
                    wait(pe, z2_stored, stored_z)
                nc.tensor.matmul(g_bank[:, 0:BD_W], x2[mb % 2][:, :], x_diag[par][:, q, :], start=True, stop=True)\
                    .then_inc(g_ready, 1)

            def pair(p, first=False, last=False, groups_done=None):
                for nb in range(PAIR_BLOCKS):
                    n, par, q = PAIR_BLOCKS * p + nb, nb // SUPER, nb % SUPER
                    s = 2 * p + par
                    tiles = [] if last and par else SLOT_TILES[q]
                    u0, upar = TILES * (s + 1), TILES * (1 - par)
                    for what, i in PE_SLOT:
                        if what == "chunk":
                            if q == 0 and i == 0:
                                wait(pe, x1lo_ready, s + 1)
                            layer1_chunk(n, nb, i)
                        elif what == "transpose" and i < len(tiles):
                            transpose_tile(u0 + tiles[i], (upar + tiles[i]) % 2, tiles[i])
                        elif what == "multiply" and i < len(tiles):
                            layer0_tile(u0 + tiles[i], (upar + tiles[i]) % 2, tiles[i], s + 1)
                        elif what == "g" and not (first and nb < LAG):
                            if q == LAG:
                                wait(pe, diag_loaded[par], 16 * BLOCK_B * (p + 1))
                            form_g(n - LAG, (nb - LAG) % PAIR_BLOCKS, groups_done if nb == 0 else None)

            def layer2(stored, width):
                wait(pe, g_stored, stored)
                for j in range(F):
                    last = nc.tensor.matmul(g_bank[:, 0:width], w2[:, j, :], g_all[:, 1 + j, 0:width],
                                            start=(j == 0), stop=(j == F - 1))
                last.then_inc(z2_ready, 1)

            pe.wait_ge(w_lo_ready, 5)
            pe.wait_ge(zeroed, 4)
            transpose_tile(0, 0, 0)
            for t in range(TILES):
                if t + 1 < TILES:
                    transpose_tile(t + 1, (t + 1) % 2, t + 1)
                layer0_tile(t, t % 2, t, 0)
            pe.wait_ge(w2_loaded, 16)
            pair(0, first=True)
            with pe.Fori(0, GROUPS - 1) as g:
                pair(2 * g + 1)
                layer2(GROUP_BLOCKS * (g + 1) - LAG, GROUP_B)
                pair(2 * g + 2, groups_done=g + 1)
            pair(PAIRS - 1, last=True)
            layer2(GROUP_BLOCKS * GROUPS - LAG, GROUP_B)
            for i in range(LAG):
                form_g(BLOCKS - LAG + i, PAIR_BLOCKS - LAG + i, GROUPS if i == 0 else None)
            layer2(BLOCKS, ZPAD)

            pe.wait_ge(top_loaded, 16 * 7)
            pe.wait_ge(z0_biased, 1)
            pe.wait_ge(z2_stored, GROUPS + 1)
            pe.wait_ge(z1_stored, GROUPS + 1)
            for i in range(8):
                half, m = divmod(i, 4)
                b = slice(half * BANK, (half + 1) * BANK)
                zb = slice(ZPAD + half * BANK, ZPAD + (half + 1) * BANK)
                operands = [(wt1[:, 0, :], z0[:, b]), (wt1[:, 1, :], z1[:, zb]), (wt1[:, 2, :], z2[:, zb]),
                            (wt1[0:D, 3, :], dense[:, b])]
                for x, (w, z) in enumerate(operands):
                    last = nc.tensor.matmul(mlp_bank(i)[:, :], w[:, m * P:(m + 1) * P], z, start=(x == 0), stop=(x == 3))
                last.then_inc(h1_ready, 1)
            for i in range(4):
                half, m = divmod(i, 2)
                b = slice(half * BANK, (half + 1) * BANK)
                pe.wait_ge(h1_stored, max(4 * (half + 1), i + 1))
                for x in range(4):
                    last = nc.tensor.matmul(mlp_bank(i)[:, :], wt2[:, x, m * P:(m + 1) * P], h1[:, x, b],
                                            start=(x == 0), stop=(x == 3))
                last.then_inc(h2_ready, 1)
            for half in range(2):
                pe.wait_ge(h2_stored, 2 * (half + 1))
                pe.wait_ge(h1_stored, 8)
                for x in range(2):
                    last = nc.tensor.matmul(mlp_bank(4 + half)[0:1, :], wt3[:, x:x + 1], h2[:, x, half * BANK:(half + 1) * BANK],
                                            start=(x == 0), stop=(x == 1))
            last.then_inc(y_ready, 1)


def kernel(**inputs):
    import numpy as np
    import concourse.bacc as bacc
    from concourse.bass_utils import run_bass_kernel_spmd

    names = [f"tbl_{i}" for i in range(F)]
    w0 = np.asarray(inputs["L0_rec_W0"]).reshape(H, F, F)
    w0_a = np.zeros((P, TILES, H), w0.dtype)
    w0_b = np.zeros((P, TILES, H), w0.dtype)
    for r in range(RS):
        t, first = r // R_TILE, r % R_TILE * F
        j = np.arange(F)
        w0_a[first:first + F, t] = w0[:, j, (j + r) % F].T
        if r:
            w0_b[first:first + F, t] = w0[:, (j + r) % F, j].T

    def by_k(w):
        return np.ascontiguousarray(np.asarray(w).reshape(H, F, H).transpose(2, 1, 0)).reshape(P, F * H)

    def by_partition(v):
        return np.ascontiguousarray(np.asarray(v).reshape(-1, P).T)

    sizes = [inputs[name].shape[0] for name in names]
    starts = np.array([sum(sizes[:i]) for i in range(F)], np.int32)

    def by_quarter(a):
        full = np.zeros((a.shape[0], SUPER_B, ROW), np.int32)
        full[:, :, :F] = a
        full = full.reshape(-1, SUPER_B, QUARTERS, GATHERS).transpose(2, 1, 0, 3)
        return np.ascontiguousarray(full)

    host = {
        "dense_t": np.ascontiguousarray(np.asarray(inputs["dense_ctx"]).T),
        "ids": by_quarter(np.asarray(inputs["ids"]).reshape(SUPERS, SUPER_B, F)).reshape(P, SUPERS * GATHERS),
        "table_starts": by_quarter(np.broadcast_to(starts, (1, SUPER_B, F))).reshape(P, GATHERS),
        "table": np.concatenate([np.asarray(inputs[name]) for name in names]),
        "w_top1": np.asarray(inputs["W_top1"]), "b_top1": by_partition(inputs["b_top1"]),
        "w_top2": np.asarray(inputs["W_top2"]), "b_top2": by_partition(inputs["b_top2"]),
        "w_top3": by_partition(inputs["W_top3"]),
        "w0_a": w0_a.reshape(P, TILES * H), "w0_b": w0_b.reshape(P, TILES * H),
        "b0": np.asarray(inputs["L0_rec_b0"]).reshape(H, 1),
        "w1_t": by_k(inputs["L0_rec_W1"]), "b1": np.asarray(inputs["L0_rec_b1"]),
        "w2_t": by_k(inputs["L0_rec_W2"]), "b2": np.asarray(inputs["L0_rec_b2"]).reshape(H, 1),
    }
    nc = bacc.Bacc("TRN2", target_bir_lowering=False, num_devices=1)

    def external(name, a):
        return nc.dram_tensor(name, a.shape, mybir.dt.from_np(a.dtype), kind="ExternalInput").ap()

    args = {name: external(name, a) for name, a in host.items()}
    out = nc.dram_tensor("out", (1, B), mybir.dt.float32, kind="ExternalOutput").ap()
    dlrm_cin_tower(nc, out=out, **args)
    result = run_bass_kernel_spmd(nc, [host], core_ids=[0])
    return result.results[0]["out"].reshape(B, 1)
```

```python
from contextlib import ExitStack

import concourse.bass as bass
from concourse import mybir

B, F, D, H = 1024, 39, 16, 128
P = 128
BLOCK_B = P // D
BLOCKS = B // BLOCK_B
SUPER = 4
SUPERS = BLOCKS // SUPER
PAIRS = SUPERS // 2
PAIR_BLOCKS = 2 * SUPER
GROUP_B = 128
GROUPS = B // GROUP_B
GROUP_BLOCKS = GROUP_B // BLOCK_B
LAG = 2
BANK = 512

RS = (F + 1) // 2
R_TILE = 3
TILES = -(-RS // R_TILE)
TILE_R = [min(R_TILE, RS - R_TILE * t) for t in range(TILES)]
SLOT_TILES = [[0, 1], [2, 3], [4, 5], [6]]

CHUNK_J = 4
CHUNKS = -(-F // CHUNK_J)
T_BANKS = 5
ACT_CHUNKS = [1, 3, 5, 7, 8]
DVE_CHUNKS = [c for c in range(CHUNKS) if c not in ACT_CHUNKS]
MACS = F - CHUNK_J * len(ACT_CHUNKS)
CHAINS = 2
FOLDS = 6
FOLD_TERMS = 4
ADDS = len(ACT_CHUNKS) - FOLD_TERMS
FOLDED = [a for a in range(len(ACT_CHUNKS)) if a % 2 == 0 or a >= 2 * ADDS]
FOLD_READ = [1, 1, 2, 3]

SUPER_B = SUPER * BLOCK_B
QUARTERS = P // SUPER_B
GATHERS = -(-F // QUARTERS)
ROW = QUARTERS * GATHERS
ROWS_MADE_BEFORE = 3
ROWS_STORED_BEFORE = 5
DIAG_AT = 1
ROWS_AT = 1
LEAD = 3

EXT = F + RS - 1
GC = F + 1
BD_W = BLOCK_B * GC

H1, H2 = 512, 256
TOP1, TOP2 = 3 * H1, (H1 // P) * H2
TOP_W = TOP1 + TOP2
ZPAD = LAG * BLOCK_B

PE_SLOT = [("chunk", 0), ("chunk", 1), ("chunk", 2), ("chunk", 3), ("chunk", 4), ("g", 0), ("chunk", 5),
           ("multiply", 0), ("chunk", 6), ("chunk", 7), ("multiply", 1), ("chunk", 8), ("chunk", 9)]
DVE_SLOT = [("chunk", 0), ("chunk", 1), ("low", 0), ("product", 0), ("add", 0), ("low", 1), ("chunk", 2),
            ("x1", 0), ("chunk", 3), ("product", 1), ("chunk", 4)]
ACT_SLOT = [("high", 0), ("chunk", 0), ("chunk", 1), ("high", 1), ("x1", 0), ("g", 0), ("chunk", 2),
            ("chunk", 3), ("chunk", 4)]


def chunk_fields(c):
    return min(CHUNK_J, F - CHUNK_J * c)


def wait(engine, semaphore, value):
    if isinstance(value, int) and value <= 0:
        return
    engine.wait_ge(semaphore, value)


def t_consumer(k_local):
    n, c = divmod(k_local, CHUNKS)
    if c in DVE_CHUNKS:
        return "dve", MACS * n + sum(chunk_fields(d) for d in DVE_CHUNKS if d <= c)
    return "act", len(ACT_CHUNKS) * n + ACT_CHUNKS.index(c) + 1


def dlrm_cin_tower(nc, dense_t, ids, table_starts, table, w_top1, b_top1, w_top2, b_top2, w_top3,
                   w0_a, w0_b, b0, w1_t, b1, w2_t, b2, out):
    f32, f32r, i32 = mybir.dt.float32, mybir.dt.float32r, mybir.dt.int32
    ALU, ACT = mybir.AluOpType, mybir.ActivationFunctionType
    AX = mybir.AxisListType

    rows_dram = nc.dram_tensor("x0_rows", (B * D, ROW), f32)[:, :]
    rows_by_block = rows_dram.rearrange("(n p) c -> p n c", p=P)
    cols_dram = nc.dram_tensor("x0_columns", (EXT, B * D), f32)[:, :]
    cols_by_super = cols_dram.rearrange("f (s b d) -> b s f d", b=SUPER_B, d=D)
    rows_by_super = rows_dram.rearrange("(s b d) c -> b s d c", b=SUPER_B, d=D)

    ctx = ExitStack()
    with ctx:
        def sb(name, shape, dt=f32):
            return ctx.enter_context(nc.sbuf_tensor(name, shape, dt))

        def sem(name):
            return ctx.enter_context(nc.semaphore(name))

        w1_hi, w1_lo = sb("w1_hi", [P, F * H], f32r), sb("w1_lo", [P, F * H], f32r)
        w2 = sb("w2", [P, F, H])
        w0_hi, w0_lo = sb("w0_hi", [P, TILES, H], f32r), sb("w0_lo", [P, TILES, H], f32r)
        top_hi, top_lo = sb("top_hi", [P, TOP_W], f32r), sb("top_lo", [P, TOP_W], f32r)
        wt3 = sb("wt3", [P, 2])
        bt1, bt2 = sb("bt1", [P, 4]), sb("bt2", [P, 2])
        b_cin = sb("b_cin", [P, 2])
        b_cin16 = sb("b_cin16", [P, 2])
        acc_start = sb("acc_start", [P, CHAINS, H])
        ids_all = sb("ids_all", [P, SUPERS, GATHERS], i32)
        starts = sb("starts", [P, GATHERS], i32)
        idx_all = sb("idx_all", [P, SUPERS + 1, GATHERS], i32)
        idx = [sb(f"idx{i}", [P, GATHERS], i32) for i in range(2)]
        emb = [sb(f"emb{i}", [P, GATHERS, D]) for i in range(2)]
        rows = [sb(f"rows{i}", [P, D, GATHERS]) for i in range(2)]
        x_scale = [sb(f"x_scale{i}", [P, SUPER, F]) for i in range(2)]
        x_diag = [sb(f"x_diag{i}", [P, SUPER, BD_W]) for i in range(2)]
        x_left = [sb(f"x_left{i}", [P, BANK]) for i in range(2)]
        dense = [x_left[half][0:3 * D, :] for half in range(2)]
        prod = [sb(f"prod{t}", [P, BANK]) for t in range(TILES)]
        pt_hi = [sb(f"pt_hi{i}", [P, BANK], f32r) for i in range(2)]
        pt_lo = [sb(f"pt_lo{i}", [P, BANK], f32r) for i in range(2)]
        x1_hi = [sb(f"x1_hi{i}", [P, BANK], f32r) for i in range(2)]
        x1_lo = [sb(f"x1_lo{i}", [P, BANK], f32r) for i in range(2)]
        w_dense = prod[TOP_W // BANK][0:3 * D, :]
        dense_split = [pt_hi[half][0:3 * D, :] for half in range(2)]
        w_dense_split = pt_lo[0][0:3 * D, :]
        acc = [sb(f"acc{i}", [P, CHAINS, H]) for i in range(2)]
        scaled = [sb(f"scaled{i}", [P, CHUNK_J * H]) for i in range(len(ACT_CHUNKS))]
        fold = sb("fold", [P, CHUNK_J * H])
        x2 = [sb(f"x2_{i}", [P, H]) for i in range(2)]
        g_all = sb("g_all", [P, GC, GROUP_B + ZPAD])
        z0 = sb("z0", [P, B])
        z1, z2 = sb("z1", [P, ZPAD + B]), sb("z2", [P, ZPAD + B])
        z_hi, z_lo = sb("z_hi", [P, 3, BANK], f32r), sb("z_lo", [P, 3, BANK], f32r)
        HID = (H1 // P) * BANK
        h1_hi, h1_lo = w1_hi[:, 0:HID], w1_lo[:, 0:HID]
        h1 = prod[0:H1 // P]
        h2 = [[prod[4], prod[5]], [prod[6], x_left[0]]]
        W1_PART = F * H // 4
        w1_stage = [g_all[:, :, :].rearrange("p a b -> p (a b)")[:, i * W1_PART:(i + 1) * W1_PART] for i in range(4)]
        w0_stage_a, w0_stage_b = z1[:, 0:TILES * H], z2[:, 0:TILES * H]
        w0_sum = z0[:, 0:TILES * H]

        t_bank = [ctx.enter_context(nc.psum_tensor(f"t_bank{i}", [P, BANK], f32)) for i in range(T_BANKS)]
        x1_bank = [ctx.enter_context(nc.psum_tensor(f"x1_bank{i}", [P, BANK], f32)) for i in range(2)]
        g_bank = ctx.enter_context(nc.psum_tensor("g_bank", [P, BANK], f32))

        ids_loaded, w0_loaded = sem("ids_loaded"), sem("w0_loaded")
        w1_loaded = sem("w1_loaded")
        bias_loaded, start_loaded = sem("bias_loaded"), sem("start_loaded")
        w2_loaded, top_loaded = sem("w2_loaded"), sem("top_loaded")
        diag_made = sem("diag_made")
        zeroed = sem("zeroed")
        idx_ready = sem("idx_ready")
        idx_all_ready = sem("idx_all_ready")
        gathered = [sem("gathered0"), sem("gathered1")]
        rows_made = sem("rows_made")
        rows_stored = [sem("rows_stored0"), sem("rows_stored1")]
        cols_stored = [sem("cols_stored0"), sem("cols_stored1")]
        left_loaded = [sem("left_loaded0"), sem("left_loaded1")]
        right_loaded = [sem(f"right_loaded{t}") for t in range(TILES)]
        scale_loaded = [sem("scale_loaded0"), sem("scale_loaded1")]
        diag_loaded = [sem("diag_loaded0"), sem("diag_loaded1")]
        b16_ready = sem("b16_ready")
        w0_summed, w_hi_ready, w_lo_ready = sem("w0_summed"), sem("w_hi_ready"), sem("w_lo_ready")
        prod_ready = sem("prod_ready")
        hi_ready, lo_ready = sem("hi_ready"), sem("lo_ready")
        l0_done = sem("l0_done")
        x1hi_ready, x1lo_ready, z0_ready = sem("x1hi_ready"), sem("x1lo_ready"), sem("z0_ready")
        t_ready = sem("t_ready")
        mac_done = sem("mac_done")
        scaled_ready = sem("scaled_ready")
        add_done = sem("add_done")
        fold_step = sem("fold_step")
        g_ready, g_stored = sem("g_ready"), sem("g_stored")
        z1_stored = sem("z1_stored")
        z2_ready, z2_stored = sem("z2_ready"), sem("z2_stored")
        split_hi_ready, split_lo_ready = sem("split_hi_ready"), sem("split_lo_ready")
        h1_hi_ready, h1_lo_ready = sem("h1_hi_ready"), sem("h1_lo_ready")
        z0_biased = sem("z0_biased")
        h1_ready, h1_stored = sem("h1_ready"), sem("h1_stored")
        h2_ready, h2_stored = sem("h2_ready"), sem("h2_stored")
        y_ready, y_stored, y_written = sem("y_ready"), sem("y_stored"), sem("y_written")

        block = ctx.enter_context(nc.Block())

        h2_bank = [t_bank[H1 // P], x1_bank[1]]
        y_bank = [x1_bank[0], g_bank]
        y = [scaled[half][0:1, :] for half in range(2)]

        def z_splits(half):
            b, zb = half * BANK, ZPAD + half * BANK
            return [(z[:, at:at + BANK], z_hi[:, i, :], z[:, at:at + BANK], z_hi[:, i, :], z_lo[:, i, :])
                    for i, (z, at) in enumerate([(z0, b), (z1, zb), (z2, zb)])]

        SPLITS = [(prod[t][:, :], top_hi[:, BANK * t:BANK * (t + 1)], prod[t][:, :],
                   top_hi[:, BANK * t:BANK * (t + 1)], top_lo[:, BANK * t:BANK * (t + 1)])
                  for t in range(TOP_W // BANK)]
        low = slice(2 * D, 3 * D)
        SPLITS.append((w_dense, w_dense_split, w_dense[low, :], w_dense_split[low, :], w_dense_split[low, :]))
        for half in range(2):
            SPLITS.append((dense[half], dense_split[half], dense[half][0:D, :], dense_split[half][0:D, :],
                           dense_split[half][0:D, :]))
        SPLITS += z_splits(0) + z_splits(1)
        SPLITS_HALF_0, SPLITS_ALL = len(SPLITS) - 3, len(SPLITS)
        SPLIT_AT = [range(0), range(0, 3), range(3, 8), range(8, SPLITS_HALF_0)]

        STORE = 16 * QUARTERS
        GATHERED = 16 * GATHERS
        COL_STORES = [(GATHERS * i, min(GATHERS, F - GATHERS * i), GATHERS * i) for i in range(QUARTERS)] + \
                     [(0, GATHERS, F), (GATHERS, EXT - F - GATHERS, F + GATHERS)]
        TOP_LOADED = 16 * 17
        COL_STORE = 16 * len(COL_STORES)

        @block.sync
        def _(sp):
            sp.dma_start(ids_all[:, :, :].rearrange("p s f -> p (s f)"), ids).then_inc(ids_loaded, 16)
            sp.dma_start(starts[:, :], table_starts).then_inc(ids_loaded, 16)
            sp.dma_start(w0_stage_a, w0_a).then_inc(w0_loaded, 16)
            sp.dma_start(w0_stage_b, w0_b).then_inc(w0_loaded, 16)
            sp.dma_start(b_cin[:, 0:1], b0).then_inc(bias_loaded, 16)
            sp.dma_start(b_cin[:, 1:2], b2).then_inc(bias_loaded, 16)
            for i in range(4):
                sp.dma_start(w1_stage[i], w1_t[:, i * W1_PART:(i + 1) * W1_PART]).then_inc(w1_loaded, 16)
            sp.wait_ge(zeroed, 1)
            sp.dma_start(acc_start[:, 0, :], b1.partition_broadcast(P)).then_inc(start_loaded, 16)

            def store_cols(s, par, turn):
                wait(sp, gathered[par], GATHERED * (turn + 1))
                for field, n, row in COL_STORES:
                    at = SUPER_B * (field // GATHERS)
                    sp.dma_start(cols_by_super[:, bass.ds(s, 1), row:row + n, :],
                                 emb[par][at:at + SUPER_B, 0:n, :].rearrange("p (o f) d -> p o f d", o=1))\
                      .then_inc(cols_stored[par], 16)

            def windows(first, count, apart, s):
                base = cols_dram[first:first + F, bass.ds(BANK * s, BANK)]
                (rs, rn), cols = base.ap
                return bass.AP(tensor=base.tensor, offset=base.offset, ap=[[apart * rs, count], [rs, rn], cols])

            def load_left(s, par, turn):
                wait(sp, cols_stored[par], COL_STORE * (turn + 1))
                sp.dma_start(x_left[par][0:R_TILE * F, :], windows(0, R_TILE, 0, s))\
                  .then_inc(left_loaded[par], 16)

            def load_right(s, t):
                sp.dma_start(prod[t][0:TILE_R[t] * F, :],
                             windows(R_TILE * t, TILE_R[t], 1, s)).then_inc(right_loaded[t], 16)

            def store_rows(s, par):
                for i in range(QUARTERS):
                    sp.dma_start(rows_by_super[:, bass.ds(s, 1), :, GATHERS * i:GATHERS * (i + 1)],
                                 rows[par][SUPER_B * i:SUPER_B * (i + 1), :, :]
                                 .rearrange("p (o d) c -> p o d c", o=1)).then_inc(rows_stored[par], 16)

            def load_scale(s, par):
                sp.dma_start(x_scale[par][:, :, :], rows_by_block[:, bass.ds(SUPER * s, SUPER), 0:F])\
                  .then_inc(scale_loaded[par], 16)

            def load_diag(s, par):
                for i in reversed(range(BLOCK_B)):
                    r = slice(D * i, D * (i + 1))
                    sp.dma_start(x_diag[par][r, :, GC * i + 1:GC * (i + 1)],
                                 rows_by_block[r, bass.ds(SUPER * s, SUPER), 0:F])\
                      .then_inc(diag_loaded[par], 16)

            def step(s, par, turn):
                store_cols(s + 2, par, turn)
                load_left(s + 2, par, turn)
                for q in range(SUPER):
                    wait(sp, lo_ready, TILES * s + SLOT_TILES[q][-1] + 1)
                    for t in SLOT_TILES[q]:
                        if t == ROWS_MADE_BEFORE:
                            wait(sp, rows_made, s + 3)
                        if t == ROWS_STORED_BEFORE:
                            wait(sp, rows_stored[par], STORE * (turn + 1))
                        load_right(s + 2, t)
                    if q == ROWS_AT:
                        store_rows(s + 2, par)
                    if q == DIAG_AT:
                        wait(sp, g_ready, SUPER * s)
                        load_diag(s + 1, 1 - par)
                wait(sp, fold_step, FOLDS * SUPER * (s + 1))
                load_scale(s + 2, par)

            store_cols(0, 0, 0)
            load_left(0, 0, 0)
            for t in range(TILES):
                load_right(0, t)
            sp.wait_ge(rows_made, 1)
            store_rows(0, 0)
            store_cols(1, 1, 0)
            sp.wait_ge(rows_stored[0], STORE)
            load_scale(0, 0)
            load_left(1, 1, 0)
            for t in range(TILES):
                sp.wait_ge(l0_done, t + 1)
                load_right(1, t)
                if t == 1:
                    sp.wait_ge(rows_made, 2)
                    store_rows(1, 1)
            sp.wait_ge(diag_made, 8)
            load_diag(0, 0)
            sp.wait_ge(rows_stored[1], STORE)
            load_scale(1, 1)
            sp.dma_start(w2[:, :, :].rearrange("p j h -> p (j h)"), w2_t).then_inc(w2_loaded, 16)
            step(0, 0, 1)
            step(1, 1, 1)
            sp.dma_start(wt3[:, :], w_top3).then_inc(top_loaded, 16)
            sp.dma_start(bt1[:, :], b_top1).then_inc(top_loaded, 16)
            sp.dma_start(bt2[:, :], b_top2).then_inc(top_loaded, 16)
            with sp.Fori(1, PAIRS - 1) as p:
                for par in range(2):
                    step(2 * p + par, par, p + 1)
            wait(sp, g_ready, SUPER * (SUPERS - 2))
            load_diag(SUPERS - 1, 1)
            sp.wait_ge(lo_ready, TILES * (SUPERS - 1))
            for t in range(3):
                sp.dma_start(prod[t][:, :], w_top1[P * t:P * (t + 1), :]).then_inc(top_loaded, 16)
            for t in range(TOP2 // BANK):
                sp.dma_start(prod[3 + t][:, :].rearrange("p (x n) -> p x n", n=H2),
                             w_top2[2 * P * t:2 * P * (t + 1), :].rearrange("(x p) n -> p x n", p=P)).then_inc(top_loaded, 16)
            for i in range(3):
                sp.dma_start(w_dense[D * i:D * (i + 1), :], w_top1[3 * P:3 * P + D, :]).then_inc(top_loaded, 16)
            for half in range(2):
                for i in range(3):
                    sp.dma_start(dense[half][D * i:D * (i + 1), :], dense_t[:, half * BANK:(half + 1) * BANK])\
                      .then_inc(top_loaded, 16)
            for par in range(2):
                sp.wait_ge(cols_stored[par], COL_STORE * PAIRS)
                sp.wait_ge(rows_stored[par], STORE * PAIRS)
            for half in range(2):
                sp.wait_ge(y_stored, half + 1)
                sp.dma_start(out[:, half * BANK:(half + 1) * BANK], y[half]).then_inc(y_written, 16)
            sp.wait_ge(y_written, 32)

        @block.gpsimd
        def _(pool):
            pool.memset(acc_start[:, :, :], 0.0).then_inc(zeroed, 1)
            pool.memset(idx_all[:, SUPERS, :], 0).then_inc(zeroed, 1)
            pool.wait_ge(zeroed, 2)
            pool.memset(x_diag[0][:, :, :], 0.0).then_inc(diag_made, 1)
            pool.wait_ge(ids_loaded, 32)
            pool.tensor_tensor(idx_all[:, 0:SUPERS, :], ids_all[:, :, :],
                               starts[:, :].unsqueeze(1).to_broadcast([P, SUPERS, GATHERS]),
                               ALU.add).then_inc(idx_all_ready, 1)
            pool.wait_ge(idx_all_ready, 1)

            def take_idx(s, par, turn):
                wait(pool, rows_made, s - 1)
                wait(pool, cols_stored[par], COL_STORE * turn)
                pool.tensor_copy(idx[par][:, :], idx_all[:, bass.ds(s, 1), :].rearrange("p g f -> p (g f)"))\
                    .then_inc(idx_ready, 1)
                wait(pool, idx_ready, s + 1)

            def gather(par, i):
                pool.indirect_dma_start(out=emb[par][:, i, :], out_offset=None, in_=table,
                                        in_offset=bass.IndirectOffsetOnAxis(ap=idx[par][:, i:i + 1], axis=0))\
                    .then_inc(gathered[par], 16)

            take_idx(0, 0, 0)
            for i in range(GATHERS):
                gather(0, i)
            pool.memset(x_diag[1][:, :, :], 0.0).then_inc(diag_made, 1)
            take_idx(1, 1, 0)
            for i in range(GATHERS):
                gather(1, i)
            for n, x in enumerate(x_diag):
                ones = x[:, :, :].rearrange("p q (b c) -> p q b c", c=GC)[:, :, :, 0]
                wait(pool, diag_made, 2 + 3 * n)
                pool.memset(ones, 1.0).then_inc(diag_made, 1)
                wait(pool, diag_made, 2 + 3 * n + 1)
                pool.affine_select(out=ones, in_=ones, compare_op=ALU.is_ge, fill=0.0, base=0,
                                   pattern=[[0, SUPER], [-D, BLOCK_B]], channel_multiplier=1).then_inc(diag_made, 1)
                wait(pool, diag_made, 2 + 3 * n + 2)
                pool.affine_select(out=ones, in_=ones, compare_op=ALU.is_ge, fill=0.0, base=D - 1,
                                   pattern=[[0, SUPER], [D, BLOCK_B]], channel_multiplier=-1).then_inc(diag_made, 1)
            pool.wait_ge(w_lo_ready, 5)
            pool.memset(g_all[:, :, 0:ZPAD], 0.0).then_inc(zeroed, 1)
            take_idx(2, 0, 1)
            for i in range(GATHERS):
                gather(0, i)

            def folds(n, nb):
                a = acc[nb % 2][:, :, :].rearrange("p c h -> p (c h)")
                s1, s2 = CHUNK_J * H // 2, CHUNK_J * H // 4
                ready = len(ACT_CHUNKS) * n
                for step in range(FOLD_TERMS - 1):
                    term, first = FOLDED[step + 1], fold if step else scaled[0]
                    if step == 0 and ADDS:
                        wait(pool, add_done, ADDS * n + 1)
                    if term < 2 * ADDS:
                        wait(pool, add_done, ADDS * n + term // 2 + 1)
                    else:
                        wait(pool, scaled_ready, ready + term + 1)
                    wait(pool, fold_step, FOLDS * n + step)
                    pool.tensor_tensor(fold[:, :], first[:, :], scaled[term][:, :], ALU.add).then_inc(fold_step, 1)
                wait(pool, fold_step, FOLDS * n + 3)
                pool.tensor_tensor(fold[:, 0:s1], fold[:, 0:s1], fold[:, s1:2 * s1], ALU.add).then_inc(fold_step, 1)
                wait(pool, mac_done, MACS * (n + 1))
                wait(pool, fold_step, FOLDS * n + 4)
                pool.tensor_tensor(fold[:, 0:s1], fold[:, 0:s1], a, ALU.add).then_inc(fold_step, 1)
                wait(pool, fold_step, FOLDS * n + 5)
                wait(pool, g_ready, n - 1)
                pool.tensor_tensor(x2[nb % 2][:, :], fold[:, 0:s2], fold[:, s2:2 * s2], ALU.add).then_inc(fold_step, 1)

            def pair(p, last=False):
                for nb in range(PAIR_BLOCKS):
                    par, q = nb // SUPER, nb % SUPER
                    to = (par + LEAD) % 2
                    if q == 0 and not last:
                        take_idx(2 * p + par + LEAD, to, p + (par + LEAD) // 2)
                    folds(PAIR_BLOCKS * p + nb, nb)
                    if not last:
                        for i in range(GATHERS * q // SUPER, GATHERS * (q + 1) // SUPER):
                            gather(to, i)

            pair(0)
            with pool.Fori(1, PAIRS - 1) as p:
                pair(p)
            pair(PAIRS - 1, last=True)
            pool.wait_ge(gathered[0], GATHERED * (PAIRS + 1))
            pool.wait_ge(gathered[1], GATHERED * PAIRS)

        @block.scalar
        def _(act):
            def make_rows(par, turn):
                wait(act, gathered[par], GATHERED * (turn + 1))
                wait(act, rows_stored[par], STORE * turn)
                nc.scalar.copy(rows[par][:, :, :], emb[par][:, :, :].rearrange("p f d -> p d f"))\
                    .then_inc(rows_made, 1)

            act.wait_ge(w0_summed, 1)
            nc.scalar.copy(w0_hi[:, :, :].rearrange("p t h -> p (t h)"), w0_sum).then_inc(w_hi_ready, 1)
            act.wait_ge(w1_loaded, 64)
            for i in range(4):
                nc.scalar.copy(w1_hi[:, i * W1_PART:(i + 1) * W1_PART], w1_stage[i]).then_inc(w_hi_ready, 1)
            make_rows(0, 0)

            def tile_hi(u, par, t):
                wait(act, prod_ready, TILES + u + 1)
                wait(act, l0_done, TILES + u - 1)
                k = TILE_R[t] * F
                nc.scalar.copy(pt_hi[par][0:k, :], prod[t][0:k, :]).then_inc(hi_ready, 1)

            def x1_high(s, par):
                wait(act, l0_done, TILES * (s + 1))
                wait(act, t_ready, CHUNKS * SUPER * (s - 1))
                nc.scalar.activation(x1_hi[par][:, :], x1_bank[par][:, :], ACT.Identity, bias=b_cin[:, 0:1])\
                    .then_inc(x1hi_ready, 1)

            def scale_chunk(n, nb, a):
                c = ACT_CHUNKS[a]
                par, q = nb // SUPER, nb % SUPER
                wait(act, t_ready, CHUNKS * n + c + 1)
                if a in FOLDED:
                    wait(act, fold_step, FOLDS * (n - 1) + FOLD_READ[FOLDED.index(a)])
                else:
                    wait(act, add_done, ADDS * (n - 1) + a // 2 + 1)
                for i in range(chunk_fields(c)):
                    j = CHUNK_J * c + i
                    last = nc.scalar.activation(scaled[a][:, i * H:(i + 1) * H],
                                                t_bank[(CHUNKS * nb + c) % T_BANKS][:, i * H:(i + 1) * H],
                                                ACT.Copy, scale=x_scale[par][:, q, j:j + 1])
                last.then_inc(scaled_ready, 1)

            def store_g(m, slot):
                wait(act, g_ready, m + 1)
                nc.scalar.copy(g_all[:, :, BLOCK_B * slot:BLOCK_B * (slot + 1)],
                               g_bank[:, 0:BD_W].rearrange("p (b c) -> p c b", c=GC)).then_inc(g_stored, 1)

            def pair(p, half, first=False, last=False):
                for nb in range(PAIR_BLOCKS):
                    n, par, q = PAIR_BLOCKS * p + nb, nb // SUPER, nb % SUPER
                    s = 2 * p + par
                    tiles = [] if last and par else SLOT_TILES[q]
                    u0 = TILES * s
                    if q == 0:
                        wait(act, scale_loaded[par], 16 * (p + 1))
                    if q == ROWS_AT and not last:
                        make_rows(par, p + 1)
                    for what, i in ACT_SLOT:
                        if what == "chunk":
                            scale_chunk(n, nb, i)
                        elif what == "high" and i < len(tiles):
                            tile_hi(u0 + tiles[i], (TILES * (1 - par) + tiles[i]) % 2, tiles[i])
                        elif what == "x1" and q == SUPER - 1 and tiles:
                            x1_high(s + 1, 1 - par)
                        elif what == "high" and last and par and i == 0:
                            split_high(SPLIT_AT[q])
                        elif what == "g" and not (first and nb < LAG):
                            store_g(n - LAG, PAIR_BLOCKS * half + nb)

            def split_high(which):
                for i in which:
                    if i == 0:
                        act.wait_ge(top_loaded, TOP_LOADED)
                        act.wait_ge(l0_done, TILES * SUPERS)
                    nc.scalar.copy(SPLITS[i][1], SPLITS[i][0]).then_inc(split_hi_ready, 1)

            def store_z(g, lo, width, stored):
                wait(act, g_stored, stored)
                nc.scalar.copy(z1[:, bass.ds(lo, width)], g_all[:, 0, 0:width]).then_inc(z1_stored, 1)
                wait(act, z2_ready, g + 1)
                nc.scalar.activation(z2[:, bass.ds(lo, width)], g_bank[:, 0:width], ACT.Identity,
                                     bias=b_cin16[:, 1:2]).then_inc(z2_stored, 1)

            def z0_bias(half):
                b = slice(half * BANK, (half + 1) * BANK)
                nc.scalar.activation(z0[:, b], z0[:, b], ACT.Identity, bias=b_cin16[:, 0:1]).then_inc(z0_biased, 1)

            def h1_relu(half, m):
                act.wait_ge(h1_ready, half * (H1 // P) + m + 1)
                if half:
                    act.wait_ge(h1_lo_ready, m + 1)
                c = slice(m * BANK, (m + 1) * BANK)
                nc.scalar.activation(h1[m][:, :], t_bank[m][:, :], ACT.Relu, bias=bt1[:, m:m + 1]).then_inc(h1_stored, 1)
                act.wait_ge(h1_stored, half * (H1 // P) + m + 1)
                nc.scalar.copy(h1_hi[:, c], h1[m][:, :]).then_inc(h1_hi_ready, 1)

            def h2_relu(half, m):
                act.wait_ge(h2_ready, half * (H2 // P) + m + 1)
                nc.scalar.activation(h2[half][m][:, :], h2_bank[m][:, :], ACT.Relu,
                                     bias=bt2[:, m:m + 1]).then_inc(h2_stored, 1)

            act.wait_ge(bias_loaded, 32)
            act.wait_ge(w_lo_ready, 5)
            make_rows(1, 0)
            x1_high(0, 0)
            act.wait_ge(zeroed, 3)
            act.wait_ge(b16_ready, 1)
            pair(0, 0, first=True)
            with act.Fori(0, GROUPS - 1) as g:
                pair(2 * g + 1, 1)
                store_z(g, GROUP_B * g, GROUP_B, GROUP_BLOCKS * (g + 1) - LAG)
                pair(2 * g + 2, 0)
            act.wait_ge(z0_ready, SUPERS // 2)
            z0_bias(0)
            pair(PAIRS - 1, 1, last=True)
            for m in range(H1 // P):
                h1_relu(0, m)
            for i in range(LAG):
                store_g(BLOCKS - LAG + i, GROUP_BLOCKS + i)
            store_z(GROUPS - 1, GROUP_B * (GROUPS - 1), GROUP_B + ZPAD, BLOCKS)
            act.wait_ge(z0_ready, SUPERS)
            z0_bias(1)
            act.wait_ge(z0_biased, 2)
            act.wait_ge(z1_stored, GROUPS)
            act.wait_ge(z2_stored, GROUPS)
            split_high(range(SPLITS_HALF_0, SPLITS_ALL))
            for m in range(H2 // P):
                h2_relu(0, m)
            for m in range(H1 // P):
                h1_relu(1, m)
            act.wait_ge(y_ready, 1)
            nc.scalar.copy(y[0], y_bank[0][0:1, :]).then_inc(y_stored, 1)
            for m in range(H2 // P):
                h2_relu(1, m)
            act.wait_ge(y_ready, 2)
            nc.scalar.copy(y[1], y_bank[1][0:1, :]).then_inc(y_stored, 1)

        @block.vector
        def _(dve):
            dve.wait_ge(bias_loaded, 32)
            nc.vector.tensor_scalar(b_cin16[:, :], b_cin[:, :], float(D), None, ALU.mult).then_inc(b16_ready, 1)
            dve.wait_ge(w0_loaded, 32)
            nc.vector.tensor_tensor(w0_sum, w0_stage_a, w0_stage_b, ALU.add).then_inc(w0_summed, 1)
            dve.wait_ge(w0_summed, 1)
            dve.wait_ge(w_hi_ready, 1)
            nc.vector.tensor_tensor(w0_lo[:, :, :].rearrange("p t h -> p (t h)"), w0_sum,
                                    w0_hi[:, :, :].rearrange("p t h -> p (t h)").bitcast(f32),
                                    ALU.subtract).then_inc(w_lo_ready, 1)
            for i in range(4):
                part = slice(i * W1_PART, (i + 1) * W1_PART)
                dve.wait_ge(w_hi_ready, i + 2)
                nc.vector.tensor_tensor(w1_lo[:, part], w1_stage[i], w1_hi[:, part].bitcast(f32),
                                        ALU.subtract).then_inc(w_lo_ready, 1)

            def product(par, t, s, turn):
                if t == 0:
                    wait(dve, left_loaded[par], 16 * (turn + 1))
                wait(dve, right_loaded[t], 16 * (s + 1))
                k = TILE_R[t] * F
                nc.vector.tensor_tensor(prod[t][0:k, :], x_left[par][0:k, :], prod[t][0:k, :], ALU.mult)\
                    .then_inc(prod_ready, 1)

            def tile_lo(u, par, t):
                wait(dve, hi_ready, u + 1)
                wait(dve, l0_done, TILES + u - 1)
                k = TILE_R[t] * F
                nc.vector.tensor_tensor(pt_lo[par][0:k, :], prod[t][0:k, :], pt_hi[par][0:k, :].bitcast(f32),
                                        ALU.subtract).then_inc(lo_ready, 1)

            def x1_low(s, par):
                wait(dve, x1hi_ready, s + 1)
                nc.vector.scalar_tensor_tensor(x1_lo[par][:, :], x1_bank[par][:, :], b_cin[:, 0:1],
                                               x1_hi[par][:, :].bitcast(f32), ALU.add, ALU.subtract)\
                    .then_inc(x1lo_ready, 1)
                nc.vector.tensor_reduce(z0[:, bass.ds(SUPER * BLOCK_B * s, SUPER * BLOCK_B)],
                                        x1_bank[par][:, :].rearrange("p (b d) -> p b d", d=D), AX.X, ALU.add)\
                    .then_inc(z0_ready, 1)

            def mac_chunk(n, nb, i):
                c = DVE_CHUNKS[i]
                par, q = nb // SUPER, nb % SUPER
                wait(dve, t_ready, CHUNKS * n + c + 1)
                if i == 0:
                    wait(dve, fold_step, FOLDS * (n - 2) + 5)
                for x in range(chunk_fields(c)):
                    e, chain = CHUNK_J * i + x, x % CHAINS
                    if e >= CHAINS:
                        wait(dve, mac_done, MACS * n + e - CHAINS + 1)
                    j = CHUNK_J * c + x
                    nc.vector.scalar_tensor_tensor(acc[nb % 2][:, chain, :],
                                                   t_bank[(CHUNKS * nb + c) % T_BANKS][:, x * H:(x + 1) * H],
                                                   x_scale[par][:, q, j:j + 1],
                                                   acc[nb % 2][:, chain, :] if e >= CHAINS else acc_start[:, chain, :],
                                                   ALU.mult, ALU.add).then_inc(mac_done, 1)

            def add_scaled(n, i):
                wait(dve, scaled_ready, len(ACT_CHUNKS) * n + 2 * (i + 1))
                nc.vector.tensor_tensor(scaled[2 * i][:, :], scaled[2 * i][:, :], scaled[2 * i + 1][:, :], ALU.add)\
                    .then_inc(add_done, 1)

            def split_low(which):
                for i in which:
                    dve.wait_ge(split_hi_ready, i + 1)
                    _, _, whole, high, low_part = SPLITS[i]
                    nc.vector.tensor_tensor(low_part, whole, high.bitcast(f32), ALU.subtract).then_inc(split_lo_ready, 1)

            def h1_low(half):
                for m in range(H1 // P):
                    c = slice(m * BANK, (m + 1) * BANK)
                    dve.wait_ge(h1_hi_ready, half * (H1 // P) + m + 1)
                    nc.vector.tensor_tensor(h1_lo[:, c], h1[m][:, :], h1_hi[:, c].bitcast(f32), ALU.subtract)\
                        .then_inc(h1_lo_ready, 1)

            def pair(p, first=False, last=False):
                for nb in range(PAIR_BLOCKS):
                    n, par, q = PAIR_BLOCKS * p + nb, nb // SUPER, nb % SUPER
                    s = 2 * p + par
                    tiles = [] if last and par else SLOT_TILES[q]
                    u0, upar = TILES * s, TILES * (1 - par)
                    s_next, q_next = (s, q + 1) if q < SUPER - 1 else (s + 1, 0)
                    par_next = par if q < SUPER - 1 else 1 - par
                    next_last = last and (par or q == SUPER - 1)
                    nxt = [] if next_last else SLOT_TILES[q_next]
                    if q == 0:
                        wait(dve, scale_loaded[par], 16 * (p + 1))

                    for what, i in DVE_SLOT:
                        if first and nb == 0 and (what, i) == ("low", 0):
                            product(1, 0, 1, 0)
                            product(1, 1, 1, 0)
                        if what == "chunk":
                            mac_chunk(n, nb, i)
                        elif what == "add" and i < ADDS:
                            add_scaled(n, i)
                        elif what == "low" and i < len(tiles):
                            tile_lo(u0 + tiles[i], (upar + tiles[i]) % 2, tiles[i])
                        elif what == "low" and last and par and i == 0:
                            split_low(SPLIT_AT[q])
                        elif what == "x1" and q == SUPER - 1 and tiles:
                            x1_low(s + 1, 1 - par)
                        elif what == "product" and i < len(nxt):
                            product(1 - par_next, nxt[i], s_next + 1, p + (par + (q == SUPER - 1) + 1) // 2)

            dve.wait_ge(start_loaded, 16)
            for t in range(TILES):
                product(0, t, 0, 0)
            x1_low(0, 0)
            pair(0, first=True)
            with dve.Fori(1, PAIRS - 1) as p:
                pair(p)
            pair(PAIRS - 1, last=True)
            h1_low(0)
            split_low(range(SPLITS_HALF_0, SPLITS_ALL))
            h1_low(1)

        @block.tensor
        def _(pe):
            def layer0_tile(u, par, t, s, xpar):
                wait(pe, lo_ready, u + 1)
                if t == 0:
                    wait(pe, z0_ready, s - 1)
                k = TILE_R[t] * F
                terms = [(w0_hi, pt_hi), (w0_lo, pt_hi), (w0_hi, pt_lo)]
                for i, (w, x) in enumerate(terms):
                    last = nc.tensor.matmul(x1_bank[xpar][:, :], w[0:k, t, :], x[par][0:k, :],
                                            start=(t == 0 and i == 0), stop=(t == TILES - 1 and i == 2))
                last.then_inc(l0_done, 1)

            def layer1_chunk(n, nb, c):
                par, q = nb // SUPER, nb % SUPER
                k_local = CHUNKS * nb + c
                bank, w = t_bank[k_local % T_BANKS], chunk_fields(c) * H
                free, count = t_consumer((k_local - T_BANKS) % (CHUNKS * PAIR_BLOCKS))
                if k_local >= T_BANKS or not isinstance(n, int) or n >= PAIR_BLOCKS:
                    per_block = MACS if free == "dve" else len(ACT_CHUNKS)
                    base = (n - nb) * per_block - (0 if k_local >= T_BANKS else PAIR_BLOCKS * per_block)
                    wait(pe, mac_done if free == "dve" else scaled_ready, base + count)
                cols, rhs = slice(q * P, (q + 1) * P), slice(CHUNK_J * c * H, CHUNK_J * c * H + w)
                terms = [(x1_hi, w1_hi), (x1_hi, w1_lo), (x1_lo, w1_hi)]
                for i, (x, wt) in enumerate(terms):
                    last = nc.tensor.matmul(bank[:, 0:w], x[par][:, cols], wt[:, rhs], start=(i == 0), stop=(i == 2))
                last.then_inc(t_ready, 1)

            def form_g(m, mb, stored_z=None):
                par, q = mb // SUPER, mb % SUPER
                wait(pe, fold_step, FOLDS * (m + 1))
                wait(pe, g_stored, m)
                if stored_z is not None:
                    wait(pe, z2_stored, stored_z)
                nc.tensor.matmul(g_bank[:, 0:BD_W], x2[mb % 2][:, :], x_diag[par][:, q, :], start=True, stop=True)\
                    .then_inc(g_ready, 1)

            def pair(p, first=False, last=False, groups_done=None):
                for nb in range(PAIR_BLOCKS):
                    n, par, q = PAIR_BLOCKS * p + nb, nb // SUPER, nb % SUPER
                    s = 2 * p + par
                    tiles = [] if last and par else SLOT_TILES[q]
                    u0, upar = TILES * s, TILES * (1 - par)
                    for what, i in PE_SLOT:
                        if what == "chunk":
                            if q == 0 and i == 0:
                                wait(pe, x1lo_ready, s + 1)
                            layer1_chunk(n, nb, i)
                        elif what == "multiply" and i < len(tiles):
                            layer0_tile(u0 + tiles[i], (upar + tiles[i]) % 2, tiles[i], s + 1, 1 - par)
                        elif what == "g" and not (first and nb < LAG):
                            if q == LAG:
                                wait(pe, diag_loaded[par], 16 * BLOCK_B * (p + 1))
                            form_g(n - LAG, (nb - LAG) % PAIR_BLOCKS, groups_done if nb == 0 else None)

            def layer2(stored, width):
                wait(pe, g_stored, stored)
                for j in range(F):
                    last = nc.tensor.matmul(g_bank[:, 0:width], w2[:, j, :], g_all[:, 1 + j, 0:width],
                                            start=(j == 0), stop=(j == F - 1))
                last.then_inc(z2_ready, 1)

            pe.wait_ge(w_lo_ready, 5)
            for t in range(TILES):
                k = TILE_R[t] * F
                pe.wait_ge(prod_ready, t + 1)
                nc.tensor.matmul(x1_bank[0][:, :], w0_sum[0:k, t * H:(t + 1) * H], prod[t][0:k, :],
                                 start=(t == 0), stop=(t == TILES - 1)).then_inc(l0_done, 1)
            pair(0, first=True)
            pe.wait_ge(w2_loaded, 16)
            with pe.Fori(0, GROUPS - 1) as g:
                pair(2 * g + 1)
                layer2(GROUP_BLOCKS * (g + 1) - LAG, GROUP_B)
                pair(2 * g + 2, groups_done=g + 1)
            pair(PAIRS - 1, last=True)

            def mlp1(half):
                pe.wait_ge(split_lo_ready, SPLITS_ALL if half else SPLITS_HALF_0)
                for m in range(H1 // P):
                    if half:
                        pe.wait_ge(h1_stored, m + 1)
                    nc.tensor.matmul(t_bank[m][:, :], w_dense_split[:, m * P:(m + 1) * P], dense_split[half],
                                     start=True, stop=False)
                    for i in range(3):
                        c = slice(H1 * i + m * P, H1 * i + (m + 1) * P)
                        terms = [(top_hi, z_hi), (top_lo, z_hi), (top_hi, z_lo)]
                        for x, (w, z) in enumerate(terms):
                            last = nc.tensor.matmul(t_bank[m][:, :], w[:, c], z[:, i, :],
                                                    start=False, stop=(i == 2 and x == 2))
                    last.then_inc(h1_ready, 1)

            def mlp2(half):
                for m in range(H2 // P):
                    if half:
                        pe.wait_ge(h2_stored, m + 1)
                    for i in range(H1 // P):
                        pe.wait_ge(h1_lo_ready, (H1 // P) * half + i + 1)
                        c = slice(TOP1 + H2 * i + m * P, TOP1 + H2 * i + (m + 1) * P)
                        terms = [(top_hi, h1_hi), (top_lo, h1_hi), (top_hi, h1_lo)]
                        for x, (w, h) in enumerate(terms):
                            last = nc.tensor.matmul(h2_bank[m][:, :], w[:, c], h[:, i * BANK:(i + 1) * BANK],
                                                    start=(i == 0 and x == 0), stop=(i == H1 // P - 1 and x == 2))
                    last.then_inc(h2_ready, 1)

            def mlp3(half):
                pe.wait_ge(h2_stored, (H2 // P) * (half + 1))
                for x in range(H2 // P):
                    last = nc.tensor.matmul(y_bank[half][0:1, :], wt3[:, x:x + 1], h2[half][x][:, :],
                                            start=(x == 0), stop=(x == H2 // P - 1))
                last.then_inc(y_ready, 1)

            pe.wait_ge(z1_stored, GROUPS - 1)
            pe.wait_ge(z2_stored, GROUPS - 1)
            pe.wait_ge(mac_done, MACS * BLOCKS)
            pe.wait_ge(scaled_ready, len(ACT_CHUNKS) * BLOCKS)
            mlp1(0)
            for i in range(LAG):
                form_g(BLOCKS - LAG + i, PAIR_BLOCKS - LAG + i)
            layer2(BLOCKS, GROUP_B + ZPAD)
            mlp2(0)
            mlp1(1)
            mlp3(0)
            mlp2(1)
            mlp3(1)


def kernel(**inputs):
    import numpy as np
    import concourse.bacc as bacc
    from concourse.bass_utils import run_bass_kernel_spmd

    names = [f"tbl_{i}" for i in range(F)]
    w0 = np.asarray(inputs["L0_rec_W0"]).reshape(H, F, F)
    w0_a = np.zeros((P, TILES, H), w0.dtype)
    w0_b = np.zeros((P, TILES, H), w0.dtype)
    for r in range(RS):
        t, first = r // R_TILE, r % R_TILE * F
        j = np.arange(F)
        w0_a[first:first + F, t] = w0[:, j, (j + r) % F].T
        if r:
            w0_b[first:first + F, t] = w0[:, (j + r) % F, j].T

    def by_k(w):
        return np.ascontiguousarray(np.asarray(w).reshape(H, F, H).transpose(2, 1, 0)).reshape(P, F * H)

    def by_partition(v):
        return np.ascontiguousarray(np.asarray(v).reshape(-1, P).T)

    sizes = [inputs[name].shape[0] for name in names]
    starts = np.array([sum(sizes[:i]) for i in range(F)], np.int32)

    def by_quarter(a):
        full = np.zeros((a.shape[0], SUPER_B, ROW), np.int32)
        full[:, :, :F] = a
        full = full.reshape(-1, SUPER_B, QUARTERS, GATHERS).transpose(2, 1, 0, 3)
        return np.ascontiguousarray(full)

    host = {
        "dense_t": np.ascontiguousarray(np.asarray(inputs["dense_ctx"]).T),
        "ids": by_quarter(np.asarray(inputs["ids"]).reshape(SUPERS, SUPER_B, F)).reshape(P, SUPERS * GATHERS),
        "table_starts": by_quarter(np.broadcast_to(starts, (1, SUPER_B, F))).reshape(P, GATHERS),
        "table": np.concatenate([np.asarray(inputs[name]) for name in names]),
        "w_top1": np.asarray(inputs["W_top1"]), "b_top1": by_partition(inputs["b_top1"]),
        "w_top2": np.asarray(inputs["W_top2"]), "b_top2": by_partition(inputs["b_top2"]),
        "w_top3": by_partition(inputs["W_top3"]),
        "w0_a": w0_a.reshape(P, TILES * H), "w0_b": w0_b.reshape(P, TILES * H),
        "b0": np.asarray(inputs["L0_rec_b0"]).reshape(H, 1),
        "w1_t": by_k(inputs["L0_rec_W1"]), "b1": np.asarray(inputs["L0_rec_b1"]),
        "w2_t": by_k(inputs["L0_rec_W2"]), "b2": np.asarray(inputs["L0_rec_b2"]).reshape(H, 1),
    }
    nc = bacc.Bacc("TRN2", target_bir_lowering=False, num_devices=1)

    def external(name, a):
        return nc.dram_tensor(name, a.shape, mybir.dt.from_np(a.dtype), kind="ExternalInput").ap()

    args = {name: external(name, a) for name, a in host.items()}
    out = nc.dram_tensor("out", (1, B), mybir.dt.float32, kind="ExternalOutput").ap()
    dlrm_cin_tower(nc, out=out, **args)
    result = run_bass_kernel_spmd(nc, [host], core_ids=[0])
    return result.results[0]["out"].reshape(B, 1)
```
